# Optimizing a Trainium2 kernel written in Bass

```python
import numpy as np
import jax
import jax.numpy as jnp

def _softmax(x, axis=-1):
    return jax.nn.softmax(x, axis=axis)

def _gelu(x):
    return jax.nn.gelu(x, approximate=True)

def _silu(x):
    return jax.nn.silu(x)

def _sigmoid(x):
    return jax.nn.sigmoid(x)

def _layernorm(x, axis=-1, eps=1e-05):
    m = jnp.mean(x, axis=axis, keepdims=True)
    v = jnp.var(x, axis=axis, keepdims=True)
    return (x - m) / jnp.sqrt(v + eps)

def _scatter_add(tgt, idx, src, axis=0):
    return tgt.at[idx].add(src)

def _segment_sum(src, seg, n):
    return jax.ops.segment_sum(src, seg, n)
kernel_name = 'mk_xattn_seq_d4_seqx_r8_c907c8'

def setup_inputs(seed: int=0):
    np.random.seed(seed)
    _w = jnp.asarray

    def _rec_inputs():
        import jax
        import jax.numpy as jnp
        _rk = jax.random.key(seed)
        x = -0.0003929 + 0.9999 * jax.random.normal(jax.random.fold_in(_rk, 1), (1, 1024, 128), jnp.float32)
        _lenS = 1024 - jax.random.randint(jax.random.fold_in(_rk, 7), (1,), 0, max(1, 1024 // 4) + 1, jnp.int32)
        _lenS2 = 6404 - jax.random.randint(jax.random.fold_in(_rk, 8), (1,), 0, max(1, 6404 // 4) + 1, jnp.int32)
        _ctx_1024P = jax.random.normal(jax.random.fold_in(_rk, 11), (1, 16, 128), jnp.float32)
        _ctx_1024c = jax.random.dirichlet(jax.random.fold_in(_rk, 511), 0.3 * jnp.ones((16,), jnp.float32), (1, 6404))
        _ctx_1024t = jnp.einsum('bsk,bkd->bsd', _ctx_1024c, _ctx_1024P)
        _ctx_1024t = _ctx_1024t * jax.lax.rsqrt(jnp.mean(jnp.square(_ctx_1024t)) + 1e-12) * 0.953939
        ctx_1024 = 2.81802e-05 + 1.00001 * (_ctx_1024t + 0.3 * jax.random.normal(jax.random.fold_in(_rk, 611), (1, 6404, 128), jnp.float32))
        itok_BxS2_4_31999 = jax.random.randint(jax.random.fold_in(_rk, 14), (1, 6404), 4, 4000, jnp.int32)
        _ctxb_2048x64P = jax.random.normal(jax.random.fold_in(_rk, 15), (1, 16, 64), jnp.float32)
        _ctxb_2048x64c = jax.random.dirichlet(jax.random.fold_in(_rk, 515), 0.3 * jnp.ones((16,), jnp.float32), (1, 6404))
        _ctxb_2048x64t = jnp.einsum('bsk,bkd->bsd', _ctxb_2048x64c, _ctxb_2048x64P)
        _ctxb_2048x64t = _ctxb_2048x64t * jax.lax.rsqrt(jnp.mean(jnp.square(_ctxb_2048x64t)) + 1e-12) * 0.953939
        ctxb_2048x64 = 0.50053 + 0.288505 * (_ctxb_2048x64t + 0.3 * jax.random.normal(jax.random.fold_in(_rk, 615), (1, 6404, 64), jnp.float32))
        _validS = jnp.arange(1024)[None, :] < _lenS[:, None]
        _validS2 = jnp.arange(6404)[None, :] < _lenS2[:, None]
        _causal = jnp.tril(jnp.ones((1024, 1024), dtype=bool))
        mask_BxS_ff1 = jnp.where(jnp.ones((1, 1024), dtype=bool), 1.0, 0.0).astype(jnp.float32)
        mask_BxS2_ik0 = jnp.where(jnp.broadcast_to(_validS2[:, :], (1, 6404)), 0, 1).astype(jnp.int32)
        return (x, ctx_1024, itok_BxS2_4_31999, ctxb_2048x64, mask_BxS_ff1, mask_BxS2_ik0)
    x, ctx_1024, itok_BxS2_4_31999, ctxb_2048x64, mask_BxS_ff1, mask_BxS2_ik0 = _rec_inputs()

    def _L0_xattn_setup():
        import jax, jax.numpy as jnp
        import numpy as np
        B, L, D = (8, 256, 128)
        key = jax.random.key(seed)
        ks = jax.random.split(key, 12)
        s = 1.0 / np.sqrt(D)
        return {'q': jax.random.normal(ks[0], (B, L, D), jnp.float32), 'k': jax.random.normal(ks[1], (B, L, D), jnp.float32), 'v': jax.random.normal(ks[2], (B, L, D), jnp.float32), 'mask': jnp.ones((B, L), jnp.float32), 'Wq': jax.random.normal(ks[3], (D, D), jnp.float32) * s, 'bq': jnp.zeros((D,), jnp.float32), 'Wk': jax.random.normal(ks[4], (D, D), jnp.float32) * s, 'bk': jnp.zeros((D,), jnp.float32), 'Wv': jax.random.normal(ks[5], (D, D), jnp.float32) * s, 'bv': jnp.zeros((D,), jnp.float32), 'Wg': jax.random.normal(ks[6], (2 * D, D), jnp.float32) * (1.0 / np.sqrt(2 * D)), 'bg': jnp.zeros((D,), jnp.float32)}
    _L0_xattn_all = _L0_xattn_setup()
    _L0_xattn_in = {k: v for k, v in _L0_xattn_all.items() if k in ('Wq', 'bq', 'Wk', 'bk', 'Wv', 'bv', 'Wg', 'bg')}
    del _L0_xattn_all

    def _L1_xattn_setup():
        import jax, jax.numpy as jnp
        import numpy as np
        E = 128
        H = 16
        D = E // H
        B, T, S = (2, 256, 256)
        SCALE = 1.0 / np.sqrt(E)

        def _layer_norm(x, g, b, eps=1e-05):
            mu = jnp.mean(x, axis=-1, keepdims=True)
            var = jnp.mean(jnp.square(x - mu), axis=-1, keepdims=True)
            return (x - mu) * jax.lax.rsqrt(var + eps) * g + b

        def _mha(h, ctx, Wq, Wk, Wv, proj_w, proj_b, causal):
            Bq, Tq, _ = h.shape
            Tk = ctx.shape[1]
            q = (h @ Wq).reshape(Bq, Tq, H, D)
            k = (ctx @ Wk).reshape(Bq, Tk, H, D)
            v = (ctx @ Wv).reshape(Bq, Tk, H, D)
            scores = jnp.einsum('bqhd,bkhd->bhqk', q, k) * SCALE
            if causal:
                mask = jnp.tril(jnp.ones((Tq, Tk), dtype=bool))
                scores = jnp.where(mask, scores, -jnp.inf)
            attn = jax.nn.softmax(scores, axis=-1)
            out = jnp.einsum('bhqk,bkhd->bqhd', attn, v).reshape(Bq, Tq, E)
            return out @ proj_w + proj_b
        key = jax.random.key(seed)
        ks = jax.random.split(key, 20)
        w = lambda k, shape: jax.random.normal(k, shape, dtype=jnp.float32) * 0.02
        inp = {'x': jax.random.normal(ks[0], (B, T, E), dtype=jnp.float32), 'context': jax.random.normal(ks[1], (B, S, E), dtype=jnp.float32), 'ln1_g': jnp.ones((E,), jnp.float32), 'ln1_b': jnp.zeros((E,), jnp.float32), 'ln2_g': jnp.ones((E,), jnp.float32), 'ln2_b': jnp.zeros((E,), jnp.float32), 'ln3_g': jnp.ones((E,), jnp.float32), 'ln3_b': jnp.zeros((E,), jnp.float32), 'Wq_s': w(ks[2], (E, E)), 'Wk_s': w(ks[3], (E, E)), 'Wv_s': w(ks[4], (E, E)), 'proj_s_w': w(ks[5], (E, E)), 'proj_s_b': jnp.zeros((E,), jnp.float32), 'Wq_c': w(ks[6], (E, E)), 'Wk_c': w(ks[7], (E, E)), 'Wv_c': w(ks[8], (E, E)), 'proj_c_w': w(ks[9], (E, E)), 'proj_c_b': jnp.zeros((E,), jnp.float32), 'w1': w(ks[10], (E, 4 * E)), 'b1': jnp.zeros((4 * E,), jnp.float32), 'w2': w(ks[11], (4 * E, E)), 'b2': jnp.zeros((E,), jnp.float32)}
        return inp
    _L1_xattn_all = _L1_xattn_setup()
    _L1_xattn_in = {k: v for k, v in _L1_xattn_all.items() if k in ('ln1_g', 'ln1_b', 'ln2_g', 'ln2_b', 'ln3_g', 'ln3_b', 'Wq_s', 'Wk_s', 'Wv_s', 'proj_s_w', 'proj_s_b', 'Wq_c', 'Wk_c', 'Wv_c', 'proj_c_w', 'proj_c_b', 'w1', 'b1', 'w2', 'b2')}
    del _L1_xattn_all

    def _L2_xattn_setup():
        import jax, jax.numpy as jnp
        import numpy as np
        H, D_MODEL, LEN_Q, LEN_K, D_K, D_V = (16, 128, 64, 256, 64, 64)
        B = 4

        def _layernorm(x, gamma, beta, eps=1e-05):
            mu = jnp.mean(x, axis=-1, keepdims=True)
            var = jnp.mean((x - mu) ** 2, axis=-1, keepdims=True)
            return (x - mu) * jax.lax.rsqrt(var + eps) * gamma + beta
        key = jax.random.key(seed)
        ks = jax.random.split(key, 16)
        s = 0.02
        return {'Q': jax.random.normal(ks[0], (B, LEN_Q, D_MODEL), jnp.float32), 'K': jax.random.normal(ks[1], (B, LEN_K, D_MODEL), jnp.float32), 'V': jax.random.normal(ks[2], (B, LEN_K, D_MODEL), jnp.float32), 'node_num': LEN_Q, 'mask': jax.random.randint(ks[3], (B, LEN_K), 0, 2, jnp.int32), 'Wq': jax.random.normal(ks[4], (D_MODEL, H * D_K), jnp.float32) * s, 'bq': jnp.zeros((H * D_K,), jnp.float32), 'Wk': jax.random.normal(ks[5], (D_MODEL, H * D_K), jnp.float32) * s, 'bk': jnp.zeros((H * D_K,), jnp.float32), 'Wv': jax.random.normal(ks[6], (D_MODEL, H * D_V), jnp.float32) * s, 'bv': jnp.zeros((H * D_V,), jnp.float32), 'Wo': jax.random.normal(ks[7], (H * D_V, D_MODEL), jnp.float32) * s, 'bo': jnp.zeros((D_MODEL,), jnp.float32), 'gamma': jnp.ones((D_MODEL,), jnp.float32), 'beta': jnp.zeros((D_MODEL,), jnp.float32)}
    _L2_xattn_all = _L2_xattn_setup()
    _L2_xattn_in = {k: v for k, v in _L2_xattn_all.items() if k in ('Wq', 'bq', 'Wk', 'bk', 'Wv', 'bv', 'Wo', 'bo', 'gamma', 'beta')}
    del _L2_xattn_all

    def _L3_xattn_setup():
        import jax, jax.numpy as jnp
        import numpy as np
        BATCH, T, H, S, P, NH = (4, 256, 128, 64, 64, 8)
        HD = H // NH

        def _layernorm(x, g, b):
            mu = jnp.mean(x, axis=-1, keepdims=True)
            var = jnp.mean((x - mu) ** 2, axis=-1, keepdims=True)
            return (x - mu) * jax.lax.rsqrt(var + 1e-05) * g + b

        def _mha(q_in, kv_in, W_qkv, b_qkv, W_o, b_o):
            Wq, Wk, Wv = jnp.split(W_qkv, 3, axis=0)
            bq, bk, bv = jnp.split(b_qkv, 3, axis=0)

            def heads(x, W, b):
                y = x @ W.T + b
                return y.reshape(y.shape[0], y.shape[1], NH, HD).transpose(0, 2, 1, 3)
            q, k, v = (heads(q_in, Wq, bq), heads(kv_in, Wk, bk), heads(kv_in, Wv, bv))
            scores = jnp.einsum('bhqd,bhkd->bhqk', q, k) * (1.0 / np.sqrt(HD))
            attn = jax.nn.softmax(scores, axis=-1)
            out = jnp.einsum('bhqk,bhkd->bhqd', attn, v)
            out = out.transpose(0, 2, 1, 3).reshape(q_in.shape)
            return out @ W_o.T + b_o
        key = jax.random.key(seed)
        ks = jax.random.split(key, 16)
        sH = 1.0 / np.sqrt(H)
        d = {}
        d['builder_state'] = jax.random.normal(ks[0], (BATCH, T, H), jnp.float32)
        d['base_state'] = jax.random.normal(ks[1], (BATCH, T, H), jnp.float32)
        d['input_ids'] = jax.random.randint(ks[2], (BATCH, T), 0, 4000)
        d['program_probs'] = jax.random.uniform(ks[3], (BATCH, T, P), jnp.float32)
        d['A'] = jax.random.normal(ks[4], (S, S), jnp.float32) * (0.5 / np.sqrt(S))
        d['Bmat'] = jax.random.normal(ks[5], (H, S), jnp.float32) * sH
        d['Cmat'] = jax.random.normal(ks[6], (S, H), jnp.float32) * (1.0 / np.sqrt(S))
        d['W_in'] = jax.random.normal(ks[7], (H, H), jnp.float32) * sH
        d['b_in'] = jnp.zeros((H,), jnp.float32)
        d['W_qkv'] = jax.random.normal(ks[8], (3 * H, H), jnp.float32) * sH
        d['b_qkv'] = jnp.zeros((3 * H,), jnp.float32)
        d['W_o'] = jax.random.normal(ks[9], (H, H), jnp.float32) * sH
        d['b_o'] = jnp.zeros((H,), jnp.float32)
        d['W_prog'] = jax.random.normal(ks[10], (H, P), jnp.float32) * (1.0 / np.sqrt(P))
        d['b_prog'] = jnp.zeros((H,), jnp.float32)
        d['g1'] = jnp.ones((H,), jnp.float32)
        d['beta1'] = jnp.zeros((H,), jnp.float32)
        d['g2'] = jnp.ones((H,), jnp.float32)
        d['beta2'] = jnp.zeros((H,), jnp.float32)
        return d
    _L3_xattn_all = _L3_xattn_setup()
    _L3_xattn_in = {k: v for k, v in _L3_xattn_all.items() if k in ('A', 'Bmat', 'Cmat', 'W_in', 'b_in', 'W_qkv', 'b_qkv', 'W_o', 'b_o', 'W_prog', 'b_prog', 'g1', 'beta1', 'g2', 'beta2')}
    del _L3_xattn_all
    return {'x': x, 'ctx_1024': ctx_1024, 'itok_BxS2_4_31999': itok_BxS2_4_31999, 'ctxb_2048x64': ctxb_2048x64, 'mask_BxS_ff1': mask_BxS_ff1, 'mask_BxS2_ik0': mask_BxS2_ik0, 'L0_xattn_Wq': _L0_xattn_in['Wq'], 'L0_xattn_bq': _L0_xattn_in['bq'], 'L0_xattn_Wk': _L0_xattn_in['Wk'], 'L0_xattn_bk': _L0_xattn_in['bk'], 'L0_xattn_Wv': _L0_xattn_in['Wv'], 'L0_xattn_bv': _L0_xattn_in['bv'], 'L0_xattn_Wg': _L0_xattn_in['Wg'], 'L0_xattn_bg': _L0_xattn_in['bg'], 'L1_xattn_ln1_g': _L1_xattn_in['ln1_g'], 'L1_xattn_ln1_b': _L1_xattn_in['ln1_b'], 'L1_xattn_ln2_g': _L1_xattn_in['ln2_g'], 'L1_xattn_ln2_b': _L1_xattn_in['ln2_b'], 'L1_xattn_ln3_g': _L1_xattn_in['ln3_g'], 'L1_xattn_ln3_b': _L1_xattn_in['ln3_b'], 'L1_xattn_Wq_s': _L1_xattn_in['Wq_s'], 'L1_xattn_Wk_s': _L1_xattn_in['Wk_s'], 'L1_xattn_Wv_s': _L1_xattn_in['Wv_s'], 'L1_xattn_proj_s_w': _L1_xattn_in['proj_s_w'], 'L1_xattn_proj_s_b': _L1_xattn_in['proj_s_b'], 'L1_xattn_Wq_c': _L1_xattn_in['Wq_c'], 'L1_xattn_Wk_c': _L1_xattn_in['Wk_c'], 'L1_xattn_Wv_c': _L1_xattn_in['Wv_c'], 'L1_xattn_proj_c_w': _L1_xattn_in['proj_c_w'], 'L1_xattn_proj_c_b': _L1_xattn_in['proj_c_b'], 'L1_xattn_w1': _L1_xattn_in['w1'], 'L1_xattn_b1': _L1_xattn_in['b1'], 'L1_xattn_w2': _L1_xattn_in['w2'], 'L1_xattn_b2': _L1_xattn_in['b2'], 'L2_xattn_Wq': _L2_xattn_in['Wq'], 'L2_xattn_bq': _L2_xattn_in['bq'], 'L2_xattn_Wk': _L2_xattn_in['Wk'], 'L2_xattn_bk': _L2_xattn_in['bk'], 'L2_xattn_Wv': _L2_xattn_in['Wv'], 'L2_xattn_bv': _L2_xattn_in['bv'], 'L2_xattn_Wo': _L2_xattn_in['Wo'], 'L2_xattn_bo': _L2_xattn_in['bo'], 'L2_xattn_gamma': _L2_xattn_in['gamma'], 'L2_xattn_beta': _L2_xattn_in['beta'], 'L3_xattn_A': _L3_xattn_in['A'], 'L3_xattn_Bmat': _L3_xattn_in['Bmat'], 'L3_xattn_Cmat': _L3_xattn_in['Cmat'], 'L3_xattn_W_in': _L3_xattn_in['W_in'], 'L3_xattn_b_in': _L3_xattn_in['b_in'], 'L3_xattn_W_qkv': _L3_xattn_in['W_qkv'], 'L3_xattn_b_qkv': _L3_xattn_in['b_qkv'], 'L3_xattn_W_o': _L3_xattn_in['W_o'], 'L3_xattn_b_o': _L3_xattn_in['b_o'], 'L3_xattn_W_prog': _L3_xattn_in['W_prog'], 'L3_xattn_b_prog': _L3_xattn_in['b_prog'], 'L3_xattn_g1': _L3_xattn_in['g1'], 'L3_xattn_beta1': _L3_xattn_in['beta1'], 'L3_xattn_g2': _L3_xattn_in['g2'], 'L3_xattn_beta2': _L3_xattn_in['beta2']}

def reference(x, ctx_1024, itok_BxS2_4_31999, ctxb_2048x64, mask_BxS_ff1, mask_BxS2_ik0, L0_xattn_Wq, L0_xattn_bq, L0_xattn_Wk, L0_xattn_bk, L0_xattn_Wv, L0_xattn_bv, L0_xattn_Wg, L0_xattn_bg, L1_xattn_ln1_g, L1_xattn_ln1_b, L1_xattn_ln2_g, L1_xattn_ln2_b, L1_xattn_ln3_g, L1_xattn_ln3_b, L1_xattn_Wq_s, L1_xattn_Wk_s, L1_xattn_Wv_s, L1_xattn_proj_s_w, L1_xattn_proj_s_b, L1_xattn_Wq_c, L1_xattn_Wk_c, L1_xattn_Wv_c, L1_xattn_proj_c_w, L1_xattn_proj_c_b, L1_xattn_w1, L1_xattn_b1, L1_xattn_w2, L1_xattn_b2, L2_xattn_Wq, L2_xattn_bq, L2_xattn_Wk, L2_xattn_bk, L2_xattn_Wv, L2_xattn_bv, L2_xattn_Wo, L2_xattn_bo, L2_xattn_gamma, L2_xattn_beta, L3_xattn_A, L3_xattn_Bmat, L3_xattn_Cmat, L3_xattn_W_in, L3_xattn_b_in, L3_xattn_W_qkv, L3_xattn_b_qkv, L3_xattn_W_o, L3_xattn_b_o, L3_xattn_W_prog, L3_xattn_b_prog, L3_xattn_g1, L3_xattn_beta1, L3_xattn_g2, L3_xattn_beta2):
    import jax
    import jax.numpy as jnp

    def _L0_xattn_ref(q, k, v, mask, Wq, bq, Wk, bk, Wv, bv, Wg, bg):
        import jax, jax.numpy as jnp
        import numpy as np
        B, L, D = (8, 256, 128)
        q0 = q
        qp = q @ Wq + bq
        kp = k @ Wk + bk
        vp = v @ Wv + bv
        scale = 1.0 / jnp.sqrt(jnp.asarray(qp.shape[-1], qp.dtype))
        w = jnp.einsum('bqd,bkd->bqk', qp, kp) * scale
        w = jax.nn.softmax(w, axis=-1)
        x = jnp.einsum('bqk,bkd->bqd', w, vp)
        gate = jnp.concatenate((qp, x), axis=-1) @ Wg + bg
        x = x * mask[..., None]
        x = x * jax.nn.sigmoid(gate)
        return x + q0

    def _L1_xattn_ref(x, context, ln1_g, ln1_b, ln2_g, ln2_b, ln3_g, ln3_b, Wq_s, Wk_s, Wv_s, proj_s_w, proj_s_b, Wq_c, Wk_c, Wv_c, proj_c_w, proj_c_b, w1, b1, w2, b2):
        import jax, jax.numpy as jnp
        import numpy as np
        E = 128
        H = 16
        D = E // H
        B, T, S = (2, 256, 256)
        SCALE = 1.0 / np.sqrt(E)

        def _layer_norm(x, g, b, eps=1e-05):
            mu = jnp.mean(x, axis=-1, keepdims=True)
            var = jnp.mean(jnp.square(x - mu), axis=-1, keepdims=True)
            return (x - mu) * jax.lax.rsqrt(var + eps) * g + b

        def _mha(h, ctx, Wq, Wk, Wv, proj_w, proj_b, causal):
            Bq, Tq, _ = h.shape
            Tk = ctx.shape[1]
            q = (h @ Wq).reshape(Bq, Tq, H, D)
            k = (ctx @ Wk).reshape(Bq, Tk, H, D)
            v = (ctx @ Wv).reshape(Bq, Tk, H, D)
            scores = jnp.einsum('bqhd,bkhd->bhqk', q, k) * SCALE
            if causal:
                mask = jnp.tril(jnp.ones((Tq, Tk), dtype=bool))
                scores = jnp.where(mask, scores, -jnp.inf)
            attn = jax.nn.softmax(scores, axis=-1)
            out = jnp.einsum('bhqk,bkhd->bqhd', attn, v).reshape(Bq, Tq, E)
            return out @ proj_w + proj_b
        x = x + _mha(_layer_norm(x, ln1_g, ln1_b), _layer_norm(x, ln1_g, ln1_b), Wq_s, Wk_s, Wv_s, proj_s_w, proj_s_b, causal=True)
        x = x + _mha(_layer_norm(x, ln2_g, ln2_b), context, Wq_c, Wk_c, Wv_c, proj_c_w, proj_c_b, causal=False)
        h = _layer_norm(x, ln3_g, ln3_b)
        x = x + (jax.nn.gelu(h @ w1 + b1, approximate=False) @ w2 + b2)
        return x

    def _L2_xattn_ref(Q, K, V, node_num, mask, Wq, bq, Wk, bk, Wv, bv, Wo, bo, gamma, beta):
        import jax, jax.numpy as jnp
        import numpy as np
        H, D_MODEL, LEN_Q, LEN_K, D_K, D_V = (16, 128, 64, 256, 64, 64)
        B = 4

        def _layernorm(x, gamma, beta, eps=1e-05):
            mu = jnp.mean(x, axis=-1, keepdims=True)
            var = jnp.mean((x - mu) ** 2, axis=-1, keepdims=True)
            return (x - mu) * jax.lax.rsqrt(var + eps) * gamma + beta
        b, lq, _ = Q.shape
        lk = K.shape[1]
        q = (Q @ Wq + bq).reshape(b, lq, H, D_K)
        k = (K @ Wk + bk).reshape(b, lk, H, D_K)
        v = (V @ Wv + bv).reshape(b, lk, H, D_V)
        scores = jnp.einsum('bqhd,bkhd->bhqk', q, k) / jnp.sqrt(jnp.float32(D_K))
        scores = jnp.where(mask[:, None, None, :] == 0, -jnp.inf, scores)
        alpha = jax.nn.softmax(scores, axis=-1)
        out = jnp.einsum('bhqk,bkhd->bqhd', alpha, v).reshape(b, lq, H * D_V)
        out = out @ Wo + bo + Q
        return _layernorm(out, gamma, beta)

    def _L3_xattn_ref(builder_state, base_state, input_ids, program_probs, A, Bmat, Cmat, W_in, b_in, W_qkv, b_qkv, W_o, b_o, W_prog, b_prog, g1, beta1, g2, beta2):
        import jax, jax.numpy as jnp
        import numpy as np
        BATCH, T, H, S, P, NH = (4, 256, 128, 64, 64, 8)
        HD = H // NH

        def _layernorm(x, g, b):
            mu = jnp.mean(x, axis=-1, keepdims=True)
            var = jnp.mean((x - mu) ** 2, axis=-1, keepdims=True)
            return (x - mu) * jax.lax.rsqrt(var + 1e-05) * g + b

        def _mha(q_in, kv_in, W_qkv, b_qkv, W_o, b_o):
            Wq, Wk, Wv = jnp.split(W_qkv, 3, axis=0)
            bq, bk, bv = jnp.split(b_qkv, 3, axis=0)

            def heads(x, W, b):
                y = x @ W.T + b
                return y.reshape(y.shape[0], y.shape[1], NH, HD).transpose(0, 2, 1, 3)
            q, k, v = (heads(q_in, Wq, bq), heads(kv_in, Wk, bk), heads(kv_in, Wv, bv))
            scores = jnp.einsum('bhqd,bhkd->bhqk', q, k) * (1.0 / np.sqrt(HD))
            attn = jax.nn.softmax(scores, axis=-1)
            out = jnp.einsum('bhqk,bhkd->bhqd', attn, v)
            out = out.transpose(0, 2, 1, 3).reshape(q_in.shape)
            return out @ W_o.T + b_o
        residual = builder_state
        x = _layernorm(builder_state, g1, beta1)
        base_n = _layernorm(base_state, g1, beta1)
        x = residual + _mha(x, base_n, W_qkv, b_qkv, W_o, b_o)
        residual = x
        xn = _layernorm(x, g2, beta2)
        U = (xn @ W_in.T + b_in) @ Bmat

        def step(s, u_t):
            s = jax.nn.silu(s @ A.T) + u_t
            return (s, s)
        _, states = jax.lax.scan(step, jnp.zeros((builder_state.shape[0], S), U.dtype), U.transpose(1, 0, 2))
        ssm_out = jnp.einsum('tbs,sh->bth', states, Cmat)
        x = residual + ssm_out
        mod = program_probs.mean(axis=1) @ W_prog.T + b_prog
        return x + mod[:, None, :]
    x = _L0_xattn_ref(x, ctx_1024, ctx_1024, mask_BxS_ff1, L0_xattn_Wq, L0_xattn_bq, L0_xattn_Wk, L0_xattn_bk, L0_xattn_Wv, L0_xattn_bv, L0_xattn_Wg, L0_xattn_bg)
    x = _L1_xattn_ref(x, ctx_1024, L1_xattn_ln1_g, L1_xattn_ln1_b, L1_xattn_ln2_g, L1_xattn_ln2_b, L1_xattn_ln3_g, L1_xattn_ln3_b, L1_xattn_Wq_s, L1_xattn_Wk_s, L1_xattn_Wv_s, L1_xattn_proj_s_w, L1_xattn_proj_s_b, L1_xattn_Wq_c, L1_xattn_Wk_c, L1_xattn_Wv_c, L1_xattn_proj_c_w, L1_xattn_proj_c_b, L1_xattn_w1, L1_xattn_b1, L1_xattn_w2, L1_xattn_b2)
    x = _L2_xattn_ref(x, ctx_1024, ctx_1024, 1024, mask_BxS2_ik0, L2_xattn_Wq, L2_xattn_bq, L2_xattn_Wk, L2_xattn_bk, L2_xattn_Wv, L2_xattn_bv, L2_xattn_Wo, L2_xattn_bo, L2_xattn_gamma, L2_xattn_beta)
    x = _L3_xattn_ref(x, ctx_1024, itok_BxS2_4_31999, ctxb_2048x64, L3_xattn_A, L3_xattn_Bmat, L3_xattn_Cmat, L3_xattn_W_in, L3_xattn_b_in, L3_xattn_W_qkv, L3_xattn_b_qkv, L3_xattn_W_o, L3_xattn_b_o, L3_xattn_W_prog, L3_xattn_b_prog, L3_xattn_g1, L3_xattn_beta1, L3_xattn_g2, L3_xattn_beta2)
    return x

_drawn_inputs = setup_inputs


def setup_inputs(seed=0):
    import zlib

    import numpy as np

    out = dict(_drawn_inputs(seed))
    spreads = {'L0_xattn_bq': (0.0, 0.8),
     'L0_xattn_bk': (0.0, 2.0),
     'L0_xattn_bv': (0.0, 0.1),
     'L0_xattn_bg': (0.0, 0.8),
     'L1_xattn_ln1_g': (1.0, 0.6),
     'L1_xattn_ln1_b': (0.0, 0.8),
     'L1_xattn_ln2_g': (1.0, 0.6),
     'L1_xattn_ln2_b': (0.0, 2.0),
     'L1_xattn_ln3_g': (1.0, 0.6),
     'L1_xattn_ln3_b': (0.0, 2.0),
     'L1_xattn_proj_s_b': (0.0, 0.1),
     'L1_xattn_proj_c_b': (0.0, 0.1),
     'L1_xattn_b1': (0.0, 0.428),
     'L1_xattn_b2': (0.0, 0.1),
     'L2_xattn_bq': (0.0, 0.8),
     'L2_xattn_bk': (0.0, 2.0),
     'L2_xattn_bv': (0.0, 0.309),
     'L2_xattn_bo': (0.0, 0.1),
     'L2_xattn_gamma': (1.0, 0.2),
     'L2_xattn_beta': (0.0, 0.1),
     'L3_xattn_b_in': (0.0, 0.1),
     'L3_xattn_b_qkv': (0.0, 0.1),
     'L3_xattn_b_o': (0.0, 0.1),
     'L3_xattn_b_prog': (0.0, 0.1),
     'L3_xattn_g1': (1.0, 0.2),
     'L3_xattn_beta1': (0.0, 0.1),
     'L3_xattn_g2': (1.0, 0.2),
     'L3_xattn_beta2': (0.0, 0.1)}
    factors = {'L1_xattn_Wq_s': 8.0,
     'L1_xattn_Wk_s': 8.0,
     'L1_xattn_Wv_s': 6.499,
     'L1_xattn_proj_s_w': 5.201,
     'L1_xattn_Wq_c': 8.0,
     'L1_xattn_Wk_c': 8.0,
     'L1_xattn_Wv_c': 2.799,
     'L1_xattn_proj_c_w': 3.101,
     'L2_xattn_Wq': 8.0,
     'L2_xattn_Wk': 8.0}
    for name, (base, spread) in spreads.items():
        noise = np.random.default_rng([zlib.crc32(name.encode()), seed]).standard_normal(out[name].shape)
        drawn = base * np.exp(spread * noise) if base else spread * noise
        out[name] = jnp.asarray(drawn.astype(out[name].dtype))
    for name, factor in factors.items():
        out[name] = (out[name] * factor).astype(out[name].dtype)
    return out
```

```python
from contextlib import ExitStack

import concourse.bass as bass
from concourse import mybir

F32 = mybir.dt.float32
F32R = mybir.dt.float32r
I32 = mybir.dt.int32
ACT = mybir.ActivationFunctionType
ALU = mybir.AluOpType
AX = mybir.AxisListType

P = 128
D = 128
NQ = 1024
QT = NQ // P
HALF = NQ // 2
NK = 6404
KT = -(-NK // P)
KPAD = KT * P
FULL = NK // P
TAIL = NK - FULL * P
CHUNK = 512
EPS = 1e-5
MASKED = -1e20
NEVER = -1e30


def chunks(n, size=CHUNK):
    return [(a, min(size, n - a)) for a in range(0, n, size)]


class Machine:

    def __init__(self, nc, ctx):
        self.nc, self.ctx, self.counts = nc, ctx, {}
        self.scores = [self.psum(f"scores{i}", [P, NQ]) for i in range(2)]
        self.work = [self.psum(f"work{i}", [P, CHUNK]) for i in range(2)]
        self.sums = [self.psum(f"sums{i}", [P, CHUNK]) for i in range(2)]
        self.x = self.sb("x", [P, QT, D])
        self.x_t = self.sb("x_t", [D, NQ])
        self.ctx_t = self.sb("ctx_t", [D, NK])
        self.ident = self.sb("ident", [P, P])
        self.neg_ident = self.sb("neg_ident", [P, P])
        self.ones = self.sb("ones", [P, P])

    def sb(self, name, shape, dt=F32, ctx=None):
        return (ctx or self.ctx).enter_context(self.nc.sbuf_tensor(name, shape, dt))

    def psum(self, name, shape):
        return self.ctx.enter_context(self.nc.psum_tensor(name, shape, F32))

    def sem(self, name):
        return self.ctx.enter_context(self.nc.semaphore(name))

    def shared(self, name, total):
        if name not in self.counts:
            self.counts[name] = [self.sem(name), 0]
        sem, before = self.counts[name]
        self.counts[name][1] += total
        return sem, before


def constants(m):
    nc = m.nc
    made = m.sem("constants_made")
    with nc.Block() as block:

        @block.gpsimd
        def _(pool):
            nc.gpsimd.memset(m.ident[:, :], 0.0).then_inc(made, 1)
            nc.gpsimd.memset(m.neg_ident[:, :], 0.0).then_inc(made, 1)
            nc.gpsimd.memset(m.ones[:, :], 1.0).then_inc(made, 1)
            pool.wait_ge(made, 3)
            for tile, value in ((m.ident, 1.0), (m.neg_ident, -1.0)):
                nc.gpsimd.affine_select(out=tile[:, :], in_=tile[:, :], compare_op=ALU.not_equal, fill=value,
                                        base=0, pattern=[[-1, P]], channel_multiplier=1).then_inc(made, 1)
            pool.wait_ge(made, 5)


def load_rows(m, tag, dram, rows, n, queue):
    full = n // P
    total = 16 * (len(chunks(full, 13)) + (n > full * P))
    loaded, count = m.shared("rows_loaded", total)
    for a, w in chunks(full, 13):
        queue.dma_start(rows[:, a:a + w, :],
                        dram[a * P:(a + w) * P, :].rearrange("(t p) d -> p t d", p=P)).then_inc(loaded, 16)
        count += 16
    if n > full * P:
        queue.dma_start(rows[0:n - full * P, full, :], dram[full * P:n, :]).then_inc(loaded, 16)
        count += 16
    return loaded, count


def turn(m, tag, rows, out_t, n, gain=None, shift=None, dram=None):
    nc = m.nc
    parts = chunks(n)
    turned, t0 = m.shared("turned", len(parts))
    copied, c0 = m.shared("turn_copied", len(parts))
    landed, l0 = m.shared("turn_landed", 1)
    with nc.Block() as block:

        @block.sync
        def _(sp):
            if dram is not None:
                loaded, count = load_rows(m, tag, dram, rows, n, sp)
                sp.wait_ge(loaded, count)
            sp.nop().then_inc(landed, 1)

        @block.tensor
        def _(pe):
            pe.wait_ge(landed, l0 + 1)
            for i, (a, w) in enumerate(parts):
                if i >= 2:
                    pe.wait_ge(copied, c0 + i - 1)
                for b, r in chunks(w, P):
                    last = nc.tensor.transpose(m.work[i % 2][:, b:b + r], rows[0:r, (a + b) // P, :],
                                               m.ident[0:r, 0:r])
                last.then_inc(turned, 1)

        @block.vector
        def _(dve):
            for i, (a, w) in enumerate(parts):
                dve.wait_ge(turned, t0 + i + 1)
                if gain is None:
                    nc.vector.tensor_copy(out_t[:, a:a + w], m.work[i % 2][:, 0:w]).then_inc(copied, 1)
                else:
                    nc.vector.tensor_scalar(out_t[:, a:a + w], m.work[i % 2][:, 0:w], gain, shift,
                                            ALU.mult, ALU.add).then_inc(copied, 1)
            dve.wait_ge(copied, c0 + len(parts))


def normalize(m, tag, rows, n, out=None):
    nc = m.nc
    out = rows if out is None else out
    tiles = -(-n // P)
    widths = [min(P, n - t * P) for t in range(tiles)]
    (got, g0), (rooted, r0) = m.shared("stats", 2 + 2 * tiles), m.shared("stats_rooted", 1)
    (inverted, i0), (scaled, s0) = m.shared("stats_inverted", 1), m.shared("rows_scaled", tiles)
    with ExitStack() as ctx:
        stats = m.sb(f"{tag}_stats_sb", [P, tiles, 6], ctx=ctx)
        mean_var = m.sb(f"{tag}_mean_var", [P, tiles, 2], ctx=ctx)
        root = m.sb(f"{tag}_root", [P, tiles], ctx=ctx)
        inverse = m.sb(f"{tag}_inverse", [P, tiles], ctx=ctx)
        eps = m.sb(f"{tag}_eps", [P, 1], ctx=ctx)
        with nc.Block() as block:

            @block.vector
            def _(dve):
                nc.vector.memset(eps[:, :], EPS).then_inc(got, 1)
                nc.vector.memset(mean_var[:, :, :], 1.0).then_inc(got, 1)
                for t, r in enumerate(widths):
                    nc.vector.bn_stats(stats[0:r, t, :], rows[0:r, t, :]).then_inc(got, 1)
                dve.wait_ge(got, g0 + 2 + tiles)
                for t, r in enumerate(widths):
                    nc.vector.bn_aggr(mean_var[0:r, t, :], stats[0:r, t, :]).then_inc(got, 1)
                dve.wait_ge(rooted, r0 + 1)
                nc.vector.reciprocal(inverse[:, :], root[:, :]).then_inc(inverted, 1)
                dve.wait_ge(inverted, i0 + 1)
                for t, r in enumerate(widths):
                    nc.vector.tensor_scalar(out[0:r, t, :], rows[0:r, t, :], mean_var[0:r, t, 0:1],
                                            inverse[0:r, t:t + 1], ALU.subtract, ALU.mult).then_inc(scaled, 1)
                dve.wait_ge(scaled, s0 + tiles)

            @block.scalar
            def _(act):
                act.wait_ge(got, g0 + 2 + 2 * tiles)
                nc.scalar.activation(root[:, :], mean_var[:, :, 1], ACT.Sqrt, bias=eps[:, :]).then_inc(rooted, 1)
                act.wait_ge(rooted, r0 + 1)


def load_columns(m, tag, pairs):
    nc = m.nc
    loaded, before = m.shared("small_loaded", 16 * len(pairs))
    with nc.Block() as block:

        @block.sync
        def _(sp):
            for dst, src in pairs:
                sp.dma_start(dst, src, allow_slow_non_contiguous=True).then_inc(loaded, 16)
            sp.wait_ge(loaded, before + 16 * len(pairs))


def column(v):
    return v.rearrange("(p a) -> p a", a=1)


def row(v):
    return v.rearrange("(a n) -> a n", a=1)


def gated_attention(m, w, scratch_ctx):
    nc = m.nc
    scale = float(D) ** -0.5
    with ExitStack() as ctx:
        sb = lambda name, shape, dt=F32: m.sb(name, shape, dt, ctx)
        wq, wk, wv = (sb(f"g_w{n}", [D, D]) for n in "qkv")
        wg = sb("g_wg", [D, 2, D])
        bq, bk = sb("g_bq", [D, 1]), sb("g_bk", [D, 1])
        bv_row, bg_row = sb("g_bv_row", [P, D]), sb("g_bg_row", [P, D])
        mask = sb("g_mask", [P, QT])
        k_a, k_b = sb("g_k_a", [D, KPAD], F32R), sb("g_k_b", [D, KPAD], F32R)
        q_a, q_b = sb("g_q_a", [D, NQ], F32R), sb("g_q_b", [D, NQ], F32R)
        q_full = sb("g_q_full", [D, NQ])
        first_row = sb("g_first_row", [P, P], F32R)
        max_row = sb("g_max_row", [P, NQ], F32R)
        v = sb("g_v", [P, KT, D])
        probs = [sb(f"g_probs{i}", [P, NQ]) for i in range(3)]
        part_max = sb("g_part_max", [P, QT, 13])
        query_max = sb("g_query_max", [P, QT])
        load_columns(m, "g_in", [(wq[:, :], w["Wq"]), (wk[:, :], w["Wk"]), (wv[:, :], w["Wv"]),
                                 (wg[:, :, :], w["Wg"].rearrange("(a p) n -> p a n", a=2)),
                                 (bq[:, :], column(w["bq"])), (bk[:, :], column(w["bk"])),
                                 (bv_row[:, :], row(w["bv"]).broadcast_to([P, D])),
                                 (bg_row[:, :], row(w["bg"]).broadcast_to([P, D])),
                                 (mask[:, :], w["mask"].rearrange("a (t p) -> p (a t)", p=P))])
        k_parts, q_parts = chunks(NK), chunks(NQ)
        v_parts = chunks(KT, 4)
        nk, nq, nv = len(k_parts), len(q_parts), len(v_parts)
        n_max = QT * nk
        cleared, filled, rounded, freed, done = (m.sem(f"g_{s}") for s in
                                                 ("cleared", "filled", "rounded", "freed", "max_done"))
        with nc.Block() as block:

            @block.gpsimd
            def _(pool):
                nc.gpsimd.memset(k_a[:, NK:KPAD].bitcast(F32), 0.0).then_inc(cleared, 1)
                nc.gpsimd.memset(k_b[:, NK:KPAD].bitcast(F32), 0.0).then_inc(cleared, 1)
                nc.gpsimd.memset(first_row[:, :].bitcast(F32), 0.0).then_inc(cleared, 1)
                nc.gpsimd.memset(max_row[:, :].bitcast(F32), 0.0).then_inc(cleared, 1)
                pool.wait_ge(cleared, 4)
                nc.gpsimd.memset(first_row[0:1, :].bitcast(F32), 1.0).then_inc(cleared, 1)
                pool.wait_ge(cleared, 5)

            @block.tensor
            def _(pe):
                u = 0

                def bank():
                    if u >= 2:
                        pe.wait_ge(freed, u - 1)
                    return m.work[u % 2]

                for a, n in k_parts:
                    nc.tensor.matmul(bank()[:, 0:n], wk[:, :], m.ctx_t[:, a:a + n], start=True,
                                     stop=True).then_inc(filled, 1)
                    u += 1
                for a, n in q_parts:
                    nc.tensor.matmul(bank()[:, 0:n], wq[:, :], m.x_t[:, a:a + n], start=True,
                                     stop=True).then_inc(filled, 1)
                    u += 1
                for t0, n in v_parts:
                    out = bank()
                    for t in range(t0, t0 + n):
                        r = P if t < FULL else TAIL
                        last = nc.tensor.matmul(out[0:r, (t - t0) * D:(t - t0 + 1) * D],
                                                m.ctx_t[:, t * P:t * P + r], wv[:, :], start=True, stop=True)
                    last.then_inc(filled, 1)
                    u += 1
                for j in range(QT):
                    for a, n in k_parts:
                        nc.tensor.matmul(bank()[:, 0:n], q_a[:, j * P:(j + 1) * P], k_a[:, a:a + n],
                                         start=True, stop=True).then_inc(filled, 1)
                        u += 1
                pe.wait_ge(done, QT)
                for h, (a, n) in enumerate(q_parts):
                    out = bank()
                    for j in range(4):
                        last = nc.tensor.matmul(out[0:1, j * P:(j + 1) * P], query_max[:, 4 * h + j:4 * h + j + 1],
                                                m.neg_ident[:, :], start=True, stop=True)
                    last.then_inc(filled, 1)
                    u += 1

            @block.scalar
            def _(act):
                for i, (a, n) in enumerate(k_parts + q_parts):
                    act.wait_ge(filled, i + 1)
                    dst, bias = (k_a, bk) if i < nk else (q_a, bq)
                    nc.scalar.activation(dst[:, a:a + n], m.work[i % 2][:, 0:n], ACT.Identity,
                                         bias=bias[:, :]).then_inc(rounded, 1)

            @block.vector
            def _(dve):
                for i, (a, n) in enumerate(k_parts + q_parts):
                    dve.wait_ge(rounded, i + 1)
                    hi, lo, bias = (k_a, k_b, bk) if i < nk else (q_a, q_b, bq)
                    if i >= nk:
                        nc.vector.tensor_scalar(q_full[:, a:a + n], m.work[i % 2][:, 0:n], bias[:, :], None,
                                                ALU.add)
                    nc.vector.scalar_tensor_tensor(out=lo[:, a:a + n], in0=m.work[i % 2][:, 0:n],
                                                   scalar=bias[:, :], in1=hi[:, a:a + n].bitcast(F32),
                                                   op0=ALU.add, op1=ALU.subtract).then_inc(freed, 1)
                u = nk + nq
                for t0, n in v_parts:
                    dve.wait_ge(filled, u + 1)
                    whole = min(n, FULL - t0)
                    if whole:
                        last = nc.vector.tensor_copy(
                            v[:, t0:t0 + whole, :],
                            m.work[u % 2][:, 0:whole * D].rearrange("p (t d) -> p t d", d=D))
                    if whole < n:
                        last = nc.vector.tensor_copy(v[0:TAIL, FULL, :],
                                                     m.work[u % 2][0:TAIL, whole * D:(whole + 1) * D])
                    last.then_inc(freed, 1)
                    u += 1
                for j in range(QT):
                    for c, (a, n) in enumerate(k_parts):
                        dve.wait_ge(filled, u + 1)
                        nc.vector.reduce_max(part_max[:, j, c:c + 1], m.work[u % 2][:, 0:n], AX.X).then_inc(freed, 1)
                        u += 1
                    dve.wait_ge(freed, u)
                    nc.vector.reduce_max(query_max[:, j:j + 1], part_max[:, j, :], AX.X).then_inc(done, 1)
                dve.wait_ge(cleared, 5)
                for h, (a, n) in enumerate(q_parts):
                    dve.wait_ge(filled, u + 1)
                    nc.vector.tensor_copy(max_row[0:1, a:a + n], m.work[u % 2][0:1, 0:n]).then_inc(freed, 1)
                    u += 1
                dve.wait_ge(freed, u)

        scored, exped, added, out_copied = (m.sem(f"g_{s}") for s in ("scored", "exped", "added", "out_copied"))
        att_t, den = q_full, sb("g_den", [P, CHUNK])
        att_t = sb("g_att_t", [D, NQ])
        with nc.Block() as block:

            @block.tensor
            def _(pe):
                def score(t):
                    if t >= 2:
                        pe.wait_ge(exped, t - 1)
                    k = slice(t * P, (t + 1) * P)
                    for h in range(2):
                        out = m.scores[t % 2][:, h * HALF:(h + 1) * HALF]
                        q = slice(h * HALF, (h + 1) * HALF)
                        nc.tensor.matmul(out, k_a[:, k], q_a[:, q], start=True, stop=False)
                        nc.tensor.matmul(out, k_b[:, k], q_a[:, q], start=False, stop=False)
                        nc.tensor.matmul(out, k_a[:, k], q_b[:, q], start=False, stop=False)
                        last = nc.tensor.matmul(out, first_row[:, :], max_row[:, q], start=False, stop=True)
                    last.then_inc(scored, 1)

                def add(t):
                    pe.wait_ge(exped, t + 1)
                    r = P if t < FULL else TAIL
                    for h in range(2):
                        p = probs[t % 3][0:r, h * HALF:(h + 1) * HALF]
                        nc.tensor.matmul(m.sums[h][:, :], v[0:r, t, :], p, start=(t == 0), stop=(t == KT - 1))
                    for h in range(2):
                        p = probs[t % 3][0:r, h * HALF:(h + 1) * HALF]
                        last = nc.tensor.matmul(m.work[0][32 * h:32 * h + 32, :], m.ones[0:r, 0:32], p,
                                                start=(t == 0), stop=(t == KT - 1))
                    last.then_inc(added, 1)

                for t in range(KT):
                    score(t)
                    if t >= 1:
                        add(t - 1)
                add(KT - 1)

            @block.scalar
            def _(act):
                for t in range(KT):
                    act.wait_ge(scored, t + 1)
                    if t >= 3:
                        act.wait_ge(added, t - 2)
                    r = P if t < FULL else TAIL
                    nc.scalar.activation(probs[t % 3][0:r, :], m.scores[t % 2][0:r, :], ACT.Exp,
                                         scale=scale).then_inc(exped, 1)

            @block.vector
            def _(dve):
                dve.wait_ge(added, KT)
                for h in range(2):
                    nc.vector.tensor_copy(att_t[:, h * HALF:(h + 1) * HALF], m.sums[h][:, :]).then_inc(out_copied, 1)
                nc.vector.tensor_copy(den[0:64, :], m.work[0][0:64, :]).then_inc(out_copied, 1)
                dve.wait_ge(out_copied, 3)

        made, taken, link, gate_read, gate_exped = (m.sem(f"g_{s}") for s in
                                                    ("made", "taken", "link", "gate_read", "gate_exped"))
        att, gate, inv = sb("g_att", [P, QT, D]), sb("g_gate", [P, QT, D]), sb("g_inv", [P, QT])
        bias_made = m.sem("g_bias_made")
        bv_cols = sb("g_bv_cols", [P, P])
        bv_col = sb("g_bv_col", [P, 1])
        gate_bias = sb("g_gate_bias", [P, D])
        load_columns(m, "g_bv", [(bv_col[:, :], column(w["bv"]))])
        with nc.Block() as block:

            @block.tensor
            def _(pe):
                pe.wait_ge(bias_made, 1)
                nc.tensor.matmul(m.scores[0][:, 0:D], bv_cols[:, :], wg[:, 1, :], start=True,
                                 stop=True).then_inc(bias_made, 1)
                for j in range(QT):
                    if j >= 2:
                        pe.wait_ge(taken, j - 1)
                    q = slice(j * P, (j + 1) * P)
                    h, c = divmod(j, 4)
                    nc.tensor.transpose(m.work[j % 2][:, 0:D], att_t[:, q], m.ident[:, :])
                    nc.tensor.matmul(m.work[j % 2][:, D:2 * D], att_t[:, q], wg[:, 1, :], start=True, stop=True)
                    nc.tensor.matmul(m.work[j % 2][:, 2 * D:2 * D + 1], den[32 * h:32 * h + 1, c * P:(c + 1) * P],
                                     m.ones[32 * h:32 * h + 1, 0:1], start=True, stop=True)
                    nc.tensor.matmul(m.sums[j % 2][:, 0:D], q_full[:, q], wg[:, 0, :], start=True,
                                     stop=True).then_inc(made, 1)

            @block.vector
            def _(dve):
                count = [0]

                def chained(ins):
                    count[0] += 1
                    ins.then_inc(link, 1)
                    dve.wait_ge(link, count[0])

                nc.vector.tensor_scalar(bv_cols[:, :], m.ones[:, :], bv_col[:, :], None,
                                        ALU.mult).then_inc(bias_made, 1)
                dve.wait_ge(bias_made, 2)
                chained(nc.vector.tensor_tensor(gate_bias[:, :], m.scores[0][:, 0:D], bg_row[:, :], ALU.add))
                for j in range(QT):
                    dve.wait_ge(made, j + 1)
                    chained(nc.vector.reciprocal(inv[:, j:j + 1], m.work[j % 2][:, 2 * D:2 * D + 1]))
                    nc.vector.scalar_tensor_tensor(out=att[:, j, :], in0=m.work[j % 2][:, 0:D],
                                                   scalar=inv[:, j:j + 1], in1=bv_row[:, :],
                                                   op0=ALU.mult, op1=ALU.add)
                    chained(nc.vector.scalar_tensor_tensor(out=gate[:, j, :], in0=m.work[j % 2][:, D:2 * D],
                                                           scalar=inv[:, j:j + 1], in1=gate_bias[:, :],
                                                           op0=ALU.mult, op1=ALU.add))
                    nc.vector.tensor_tensor(gate[:, j, :], m.sums[j % 2][:, 0:D], gate[:, j, :],
                                            ALU.add).then_inc(taken, 1)
                dve.wait_ge(taken, QT)
                nc.vector.nop().then_inc(gate_read, 1)
                dve.wait_ge(gate_exped, 1)
                chained(nc.vector.tensor_scalar(gate[:, :, :], gate[:, :, :], 1.0, None, ALU.add))
                chained(nc.vector.reciprocal(gate[:, :, :], gate[:, :, :]))
                for j in range(QT):
                    last = nc.vector.tensor_scalar(att[:, j, :], att[:, j, :], mask[:, j:j + 1], None, ALU.mult)
                chained(last)
                chained(nc.vector.tensor_tensor(att[:, :, :], att[:, :, :], gate[:, :, :], ALU.mult))
                chained(nc.vector.tensor_tensor(m.x[:, :, :], att[:, :, :], m.x[:, :, :], ALU.add))

            @block.scalar
            def _(act):
                act.wait_ge(gate_read, 1)
                nc.scalar.activation(gate[:, :, :], gate[:, :, :], ACT.Exp, scale=-1.0).then_inc(gate_exped, 1)
                act.wait_ge(gate_exped, 1)


class Heads:

    def __init__(self, tag, heads, d, keys, scale, causal=False, masked=False):
        self.tag, self.heads, self.d, self.keys, self.scale = tag, heads, d, keys, scale
        self.causal, self.masked = causal, masked
        self.wide = d == 64
        self.blocks = [0, 64] if self.wide else [0, 32, 64]
        self.max_at = 64 if self.wide else 96
        self.tiles = -(-keys // P)
        self.k_parts, self.q_parts = chunks(keys), chunks(NQ)
        self.v_parts = chunks(self.tiles, CHUNK // d if self.wide else 32)
        self.max_parts = [(j, c, a, n) for j in range(QT)
                          for c, (a, n) in enumerate(chunks((j + 1) * P if causal else keys))]
        self.n_probs = 2 if self.wide else 3
        self.out_units = [("out", c, list(range(a, a + n)), None) for c, (a, n) in enumerate(chunks(QT, 2))]
        prep = [("k", i, a, n) for i, (a, n) in enumerate(self.k_parts)]
        prep += [("q", i, a, n) for i, (a, n) in enumerate(self.q_parts)]
        if self.wide:
            prep += [("v", i, a, n) for i, (a, n) in enumerate(self.v_parts)]
        self.n_split = len(self.k_parts) + len(self.q_parts)
        prep += [("max", j, c, (a, n)) for j, c, a, n in self.max_parts]
        prep += [("row", i, a, n) for i, (a, n) in enumerate(self.q_parts)]
        self.prep_units = prep

    def rows(self, t):
        return min(P, self.keys - t * P)

    def first_query(self, t):
        return P * t if self.causal and t >= 2 else 0

    def last_chunk(self, j, c):
        return c == max(cc for jj, cc, _, _ in self.max_parts if jj == j)


def all_values(m, tag, dram, wv, key_t, v_all, keys):
    nc = m.nc
    tiles, width = -(-keys // P), wv.shape[1]
    parts = chunks(tiles, CHUNK // width)
    made, taken, loaded = (m.sem(f"{tag}_v_{n}") for n in ("made", "taken", "loaded"))
    with nc.Block() as block:

        @block.sync
        def _(sp):
            sp.dma_start(wv[:, :], dram).then_inc(loaded, 16)

        @block.tensor
        def _(pe):
            pe.wait_ge(loaded, 16)
            for i, (a, n) in enumerate(parts):
                if i >= 2:
                    pe.wait_ge(taken, i)
                for t in range(a, a + n):
                    r = min(P, keys - t * P)
                    last = nc.tensor.matmul(m.work[i % 2][0:r, (t - a) * width:(t - a + 1) * width],
                                            key_t[:, t * P:t * P + r], wv[:, :], start=True, stop=True)
                last.then_inc(made, 1)

        @block.vector
        def _(dve):
            nc.vector.memset(v_all[:, tiles - 1, :], 0.0).then_inc(taken, 1)
            dve.wait_ge(taken, 1)
            for i, (a, n) in enumerate(parts):
                dve.wait_ge(made, i + 1)
                whole = min(n, keys // P - a)
                if whole:
                    last = nc.vector.tensor_copy(v_all[:, a:a + whole, :],
                                                 m.work[i % 2][:, 0:whole * width].rearrange("p (t w) -> p t w", w=width))
                if whole < n:
                    r = keys - (a + whole) * P
                    last = nc.vector.tensor_copy(v_all[0:r, a + whole, :],
                                                 m.work[i % 2][0:r, whole * width:(whole + 1) * width])
                last.then_inc(taken, 1)
            dve.wait_ge(taken, len(parts) + 1)


def head_attention(m, s, w, key_t, query_t, masks=None):
    nc, tag, d = m.nc, s.tag, s.d
    H, NT = s.heads, s.tiles
    with ExitStack() as ctx:
        sb = lambda name, shape, dt=F32: m.sb(f"{tag}_{name}", shape, dt, ctx)
        keys_w = NT * P
        k_s = [sb(f"k{i}", [P, keys_w], F32R) for i in range(2)]
        q_s = [sb(f"q{i}", [P, NQ], F32R) for i in range(2)]
        if s.wide:
            k2_s = [sb(f"k2{i}", [P, keys_w], F32R) for i in range(2)]
            q2_s = [sb(f"q2{i}", [P, NQ], F32R) for i in range(2)]
            qm_s = [sb(f"qm{i}", [P, NQ], F32R) for i in range(2)]
            passes = [(k_s, q_s), (k2_s, q2_s)]
            max_q, max_k, row_q = qm_s, k2_s, q2_s
            den_s = sb("den", [P, CHUNK])
            mask_int, mask_bias = sb("mask_int", [P, NT], I32), sb("mask_bias", [P, NT])
        else:
            passes = [(k_s, q_s)]
            max_q, max_k, row_q = q_s, k_s, q_s
        v_w = 64 if s.wide else 32
        v_s = [sb(f"v{i}", [P, NT, v_w]) for i in range(2)]
        probs = [sb(f"probs{i}", [P, NQ]) for i in range(s.n_probs)]
        wk_s, wq_s = ([sb(f"{n}{i}", [D, P]) for i in range(2)] for n in ("wk", "wq"))
        if s.wide:
            wv_s = [sb(f"wv{i}", [D, d]) for i in range(2)]
        else:
            v_all, wv = sb("v_all", [P, NT, H * d]), sb("wv", [D, H * d])
        bk_s, bq_s = ([sb(f"{n}{i}", [P, 1]) for i in range(2)] for n in ("bk", "bq"))
        wo_s = [sb(f"wo{i}", [P, D + 1]) for i in range(2)]
        acc_s = sb("acc", [P, CHUNK])
        part_max = sb("part_max", [P, QT, 13])
        query_max = sb("query_max", [P, QT])
        inv = sb("inv", [P, QT])

        sem = lambda name: m.sem(f"{tag}_{name}")
        cleared, mask_in, mask_done = sem("cleared"), sem("mask_in"), sem("mask_done")
        mask_zero, keys_in = sem("mask_zero"), sem("keys_in")
        staged, out_staged = ([sem(f"{n}staged{i}") for i in range(2)] for n in ("", "out_"))
        filled, rounded, freed = (sem(n) for n in ("filled", "rounded", "freed"))
        tile_max, max_done, inverted = sem("tile_max"), sem("max_done"), sem("inverted")
        scored, exped, added, acc_taken = (sem(n) for n in ("scored", "exped", "added", "acc_taken"))

        with nc.Block() as block:

            @block.gpsimd
            def _(pool):
                n = 0

                def put(value, ap):
                    nonlocal n
                    nc.gpsimd.memset(ap, value).then_inc(cleared, 1)
                    n += 1
                    pool.wait_ge(cleared, n)

                whole = s.keys // P
                if s.masked:
                    nc.gpsimd.memset(mask_int[:, :], 0).then_inc(mask_zero, 1)
                for i in range(2):
                    for t in (wk_s[i], wq_s[i], bk_s[i], bq_s[i], wo_s[i]):
                        put(0.0, t[:, :])
                for i in range(2):
                    if whole < NT:
                        put(0.0, k_s[i][:, s.keys:keys_w].bitcast(F32))
                    if s.wide:
                        for t in (k2_s[i], q2_s[i], qm_s[i]):
                            put(0.0, t[:, :].bitcast(F32))
                        for at in (0, 32, 64, 96):
                            put(1.0, wo_s[i][at:at + 1, D:D + 1])
                        put(1.0, k2_s[i][64:65, :].bitcast(F32))
                        put(1.0, qm_s[i][96:97, :].bitcast(F32))
                        if whole < NT:
                            put(0.0, v_s[i][:, whole, :])
                    else:
                        put(1.0, bk_s[i][96:97, :])
                        put(0.0, v_s[i][:, :, :])
                        put(1.0, v_s[i][:, 0:whole, d:d + 1])
                        if whole < NT:
                            put(1.0, v_s[i][0:s.rows(whole), whole, d:d + 1])

            if not s.wide:

                @block.sync
                def _(sp):
                    sp.wait_ge(cleared, 10)
                    for i in range(2):
                        for at in (0, 32, 64, 96):
                            sp.dma_start(wo_s[i][at + d:at + d + 1, D:D + 1], m.ones[0:1, 0:1]).then_inc(mask_in, 16)
                    sp.wait_ge(mask_in, 16 * 8)

        if s.masked:
            with nc.Block() as block:

                @block.sync
                def _(sp):
                    whole = s.keys // P
                    sp.dma_start(mask_int[:, 0:whole], masks[0, 0:whole * P].rearrange("(t p) -> p t", p=P),
                                 allow_slow_non_contiguous=True).then_inc(keys_in, 16)
                    sp.dma_start(mask_int[0:s.rows(whole), whole:NT], column(masks[0, whole * P:s.keys]),
                                 allow_slow_non_contiguous=True).then_inc(keys_in, 16)
                    for i, (a, n) in enumerate(chunks(s.keys, NQ)):
                        if i >= 2:
                            sp.wait_ge(mask_done, i - 1)
                        sp.dma_start(probs[i % 2][96:97, 0:n].bitcast(I32), masks[:, a:a + n]).then_inc(mask_in, 16)
                        sp.wait_ge(mask_in, 16 * (i + 1))

                @block.vector
                def _(dve):
                    for i, (a, n) in enumerate(chunks(s.keys, NQ)):
                        dve.wait_ge(mask_in, 16 * (i + 1))
                        for b in range(2):
                            last = nc.vector.tensor_scalar(k2_s[b][96:97, a:a + n], probs[i % 2][96:97, 0:n].bitcast(I32),
                                                           0.0, MASKED, ALU.is_equal, ALU.mult)
                        last.then_inc(mask_done, 1)
                    dve.wait_ge(keys_in, 32)
                    nc.vector.tensor_scalar(mask_bias[:, :], mask_int[:, :], 0.0, NEVER, ALU.is_equal,
                                            ALU.mult).then_inc(mask_done, 1)
                    dve.wait_ge(mask_done, i + 2)

        if not s.wide:
            all_values(m, tag, w["Wv"], wv, key_t, v_all, s.keys)

        stage_dmas = 2 * len(s.blocks) + (1 if s.wide else 0)
        out_dmas = 2 if s.wide else 4
        if w["bq"] is not None:
            stage_dmas += 2 * len(s.blocks)

        work = m.work if s.wide else m.work + [m.sums[1]]
        NW = len(work)

        U = len(s.out_units) + len(s.prep_units)
        UP = len(s.prep_units)
        first_out = len(s.out_units)

        def unit_base(h):
            return UP if isinstance(h, int) and h == 0 else 2 * UP + (h - 1) * U

        def step_units(h_is_first, has_next):
            units = ([] if h_is_first else s.out_units) + (s.prep_units if has_next is not None else [])
            slots = [[] for _ in range(NT)]
            for u, unit in enumerate(units):
                slots[u * (NT - 1) // len(units)].append((u, unit))
            return slots

        def prev_user(t, ring):
            return t - ring if t >= ring else max(x for x in range(NT) if x % ring == t % ring) - NT

        def run(engine, prepare, step, finish):
            prepare()
            step(0, 0, True, 1)
            with engine.Fori(0, (H - 2) // 2) as i:
                step(2 * i + 1, 1, False, i + 2)
                step(2 * i + 2, 0, False, i + 2)
            step(H - 1, 1, False, None)
            finish()

        with nc.Block() as block:

            @block.sync
            def _(sp):
                def stage(h, par):
                    cols = bass.ds(h * d, d)
                    for at in s.blocks:
                        sp.dma_start(wk_s[par][:, at:at + d], w["Wk"][:, cols]).then_inc(staged[par], 16)
                        sp.dma_start(wq_s[par][:, at:at + d], w["Wq"][:, cols]).then_inc(staged[par], 16)
                        if w["bq"] is not None:
                            sp.dma_start(bk_s[par][at:at + d, :], column(w["bk"])[cols, :]).then_inc(staged[par], 16)
                            sp.dma_start(bq_s[par][at:at + d, :], column(w["bq"])[cols, :]).then_inc(staged[par], 16)
                    if s.wide:
                        sp.dma_start(wv_s[par][:, :], w["Wv"][:, cols]).then_inc(staged[par], 16)

                def stage_out(h, par):
                    for at in ((0, 64) if s.wide else (0, 32, 64, 96)):
                        sp.dma_start(wo_s[par][at:at + d, 0:D],
                                     w["Wo"][bass.ds(h * d, d), :]).then_inc(out_staged[par], 16)

                stage(0, 0)
                stage(1, 1)
                stage_out(0, 0)
                stage_out(1, 1)
                sp.wait_ge(freed, UP)
                stage(2, 0)

                def step(h, par, more):
                    sp.wait_ge(freed, unit_base(h))
                    if more:
                        stage(h + 2, par)
                    sp.wait_ge(freed, unit_base(h) + first_out)
                    stage_out(h + 1, 1 - par)

                with sp.Fori(0, (H - 4) // 2) as i:
                    step(2 * i + 1, 1, True)
                    step(2 * i + 2, 0, True)
                step(H - 3, 1, True)
                step(H - 2, 0, False)
                for par in range(2):
                    sp.wait_ge(staged[par], 16 * stage_dmas * (H // 2))
                    sp.wait_ge(out_staged[par], 16 * out_dmas * (H // 2))

            @block.tensor
            def _(pe):
                def fill(unit, base, u, par, h, nth=0):
                    kind, i, a, n = unit
                    bank = work[u % NW]
                    if u >= NW:
                        pe.wait_ge(freed, base + u - NW + 1)
                    if kind == "out":
                        if i == 0:
                            pe.wait_ge(out_staged[par], 16 * out_dmas * nth)
                            pe.wait_ge(acc_taken, h + 1)
                        for g, j in enumerate(a):
                            half, c = divmod(j, 4)
                            r = slice(64 * half, 64 * half + 64)
                            o = g * (D + 1)
                            if s.wide:
                                nc.tensor.matmul(bank[:, o:o + D], acc_s[r, c * P:(c + 1) * P], wo_s[par][r, 0:D],
                                                 start=True, stop=True)
                                last = nc.tensor.matmul(bank[:, o + D:o + D + 1], den_s[r, c * P:(c + 1) * P],
                                                        wo_s[par][r, D:D + 1], start=True, stop=True)
                            else:
                                last = nc.tensor.matmul(bank[:, o:o + D + 1], acc_s[r, c * P:(c + 1) * P],
                                                        wo_s[par][r, :], start=True, stop=True)
                    elif kind == "k":
                        if i == 0:
                            pe.wait_ge(staged[par], 16 * stage_dmas * nth)
                        last = nc.tensor.matmul(bank[:, 0:n], wk_s[par][:, :], key_t[:, a:a + n], start=True, stop=True)
                    elif kind == "q":
                        last = nc.tensor.matmul(bank[:, 0:n], wq_s[par][:, :], query_t[:, a:a + n], start=True, stop=True)
                    elif kind == "v":
                        for t in range(a, a + n):
                            r = s.rows(t)
                            last = nc.tensor.matmul(bank[0:r, (t - a) * d:(t - a + 1) * d], key_t[:, t * P:t * P + r],
                                                    wv_s[par][:, :], start=True, stop=True)
                    elif kind == "max":
                        j, c, (a, n) = i, a, n
                        if j == 0 and c == 0:
                            pe.wait_ge(freed, base + u)
                        edge = s.causal and s.last_chunk(j, c)
                        last = nc.tensor.matmul(bank[:, 0:n], max_q[par][:, j * P:(j + 1) * P],
                                                max_k[par][:, a:a + n], start=True, stop=not edge)
                        if edge:
                            last = nc.tensor.matmul(bank[:, n - P:n], m.ident[:, :], masks["later_key"][:, :],
                                                    start=False, stop=True)
                    else:
                        if i == 0:
                            pe.wait_ge(max_done, QT * (h + 1))
                        for c in range(4):
                            j = 4 * i + c
                            last = nc.tensor.matmul(bank[s.max_at:s.max_at + 1, c * P:(c + 1) * P],
                                                    query_max[:, j:j + 1], m.neg_ident[:, :], start=True, stop=True)
                    last.then_inc(filled, 1)

                def score(h, par, t, half):
                    prev = prev_user(t, 2)
                    first = half == (1 if s.first_query(t) >= HALF else 0)
                    if first and not (isinstance(h, int) and h == 0 and prev < 0):
                        pe.wait_ge(exped, h * NT + prev + 1)
                    a, b = max(s.first_query(t), half * HALF), (half + 1) * HALF
                    if a >= b:
                        return
                    out = m.scores[t % 2][:, a:b]
                    diagonal = s.causal and half * HALF <= t * P < b
                    for n, (ks, qs) in enumerate(passes):
                        last = nc.tensor.matmul(out, ks[par][:, t * P:(t + 1) * P], qs[par][:, a:b],
                                                start=(n == 0), stop=(n == len(passes) - 1 and not diagonal))
                    if s.causal and t == 1 and half == 0:
                        nc.tensor.matmul(m.scores[t % 2][:, 0:P], m.ident[:, :], masks["all"][:, :],
                                         start=False, stop=False)
                    if diagonal:
                        last = nc.tensor.matmul(m.scores[t % 2][:, t * P:(t + 1) * P], m.ident[:, :],
                                                masks["earlier_query"][:, :], start=False, stop=True)
                    if half == 1:
                        last.then_inc(scored, 1)

                def add(h, par, t, part):
                    if part == 0:
                        pe.wait_ge(exped, h * NT + t + 1)
                        if t == 0 and not (isinstance(h, int) and h == 0):
                            pe.wait_ge(acc_taken, h)
                    if part < 2:
                        half = part
                        a, b = max(s.first_query(t), half * HALF), (half + 1) * HALF
                        if a >= b:
                            return
                        p = probs[t % s.n_probs][:, a:b]
                        o = slice(a - half * HALF, b - half * HALF)
                        tiles = [x for x in range(NT) if s.first_query(x) < b]
                        ends = t in tiles[-2:]
                        if s.wide:
                            last = nc.tensor.matmul(m.sums[0][64 * half:64 * half + 64, o], v_s[par][:, t, :], p,
                                                    start=(t == 0), stop=(t == NT - 1))
                        else:
                            at = 64 * half + 32 * (t % 2)
                            last = nc.tensor.matmul(m.sums[0][at:at + 32, o], v_s[par][:, t, :], p,
                                                    start=(t < 2), stop=ends)
                    else:
                        for half in range(2):
                            at = 64 * half + 32 * (t % 2)
                            last = nc.tensor.matmul(m.sums[1][at:at + 32, :], m.ones[:, 0:32],
                                                    probs[t % s.n_probs][:, half * HALF:(half + 1) * HALF],
                                                    start=(t < 2), stop=(t >= NT - 2))
                    if part == (2 if s.wide else 1):
                        last.then_inc(added, 1)

                def prepare():
                    for u, unit in enumerate(s.prep_units):
                        fill(unit, 0, u, 0, 0, 1)

                def step(h, par, is_first, has_next):
                    base = unit_base(h)
                    slots = step_units(is_first, has_next)
                    pe.wait_ge(freed, base)
                    for t in range(NT + 1):
                        own = [(score, t, half) for half in range(2)] if t < NT else []
                        own += [(add, t - 1, part) for part in range(3 if s.wide else 2)] if t >= 1 else []
                        units = slots[t] if t < NT else []
                        for k, (what, tile, part) in enumerate(own):
                            what(h, par, tile, part)
                            for u, unit in units[k * len(units) // len(own):(k + 1) * len(units) // len(own)]:
                                if unit[0] == "out":
                                    fill(unit, base, u, 1 - par, h - 1, H // 2 if has_next is None else has_next - 1)
                                else:
                                    fill(unit, base, u, 1 - par, h + 1, has_next)

                def finish():
                    base = unit_base(H - 1) + first_out
                    for u, unit in enumerate(s.out_units):
                        fill(unit, base, u, 1, H - 1, H // 2)

                run(pe, prepare, step, finish)

            @block.scalar
            def _(act):
                def split_count(h):
                    return s.n_split * h

                def take(unit, base, u, par, h):
                    kind, i, a, n = unit
                    if kind not in "kq":
                        return
                    act.wait_ge(filled, base + u + 1)
                    dst, bias = (k_s, bk_s) if kind == "k" else (q_s, bq_s)
                    if s.wide:
                        again = k2_s if kind == "k" else qm_s
                        nc.scalar.activation(again[par][0:64, a:a + n], work[u % NW][0:64, 0:n], ACT.Identity,
                                             bias=bias[par][0:64, :])
                    nc.scalar.activation(dst[par][:, a:a + n], work[u % NW][:, 0:n], ACT.Identity,
                                         bias=bias[par][:, :]).then_inc(rounded, 1)

                def prepare():
                    for u, unit in enumerate(s.prep_units):
                        take(unit, 0, u, 0, 0)

                def step(h, par, is_first, has_next):
                    base = unit_base(h)
                    slots = step_units(is_first, has_next)
                    for t in range(NT):
                        act.wait_ge(scored, h * NT + t + 1)
                        prev = prev_user(t, s.n_probs)
                        if not (isinstance(h, int) and h == 0 and prev < 0):
                            act.wait_ge(added, h * NT + prev + 1)
                        q0 = s.first_query(t)
                        nc.scalar.activation(probs[t % s.n_probs][:, q0:NQ], m.scores[t % 2][:, q0:NQ], ACT.Exp,
                                             bias=mask_bias[:, t:t + 1] if s.masked else 0.0,
                                             scale=s.scale).then_inc(exped, 1)
                        for u, unit in slots[t]:
                            take(unit, base, u, 1 - par, h + 1)
                    act.wait_ge(added, (h + 1) * NT)
                    if not is_first:
                        act.wait_ge(freed, base + first_out)
                    if s.wide:
                        nc.scalar.activation(den_s[:, :], m.sums[1][:, :], ACT.Copy)
                    nc.scalar.activation(acc_s[:, :], m.sums[0][:, :], ACT.Copy).then_inc(acc_taken, 1)

                run(act, prepare, step, lambda: None)

            @block.vector
            def _(dve):
                def take(unit, base, u, par, h):
                    kind, i, a, n = unit
                    bank = work[u % NW]
                    if kind in "kq":
                        dve.wait_ge(rounded, s.n_split * h + i + 1 + (len(s.k_parts) if kind == "q" else 0))
                        bias = bk_s if kind == "k" else bq_s
                        hi = (k_s if kind == "k" else q_s)[par]
                        if s.wide and kind == "q":
                            lo, r = q2_s[par], slice(0, 64)
                        else:
                            lo, r = hi, slice(64, 128 if s.wide else 96) if kind == "k" else slice(32, 64)
                        last = nc.vector.scalar_tensor_tensor(out=lo[r, a:a + n], in0=bank[r, 0:n], scalar=bias[par][r, :],
                                                              in1=hi[r, a:a + n].bitcast(F32), op0=ALU.add,
                                                              op1=ALU.subtract)
                        if not s.wide and kind == "q" and i == len(s.q_parts) - 1:
                            last = nc.vector.tensor_copy(v_s[par][:, :, 0:d], v_all[:, :, bass.ds(h * d, d)])
                    elif kind == "v":
                        dve.wait_ge(filled, base + u + 1)
                        whole = min(n, s.keys // P - a)
                        if whole:
                            last = nc.vector.tensor_copy(v_s[par][:, a:a + whole, 0:d],
                                                         bank[:, 0:whole * d].rearrange("p (t d) -> p t d", d=d))
                        if whole < n:
                            r = s.rows(a + whole)
                            last = nc.vector.tensor_copy(v_s[par][0:r, a + whole, 0:d],
                                                         bank[0:r, whole * d:(whole + 1) * d])
                    elif kind == "max":
                        j, c, (a, n) = i, a, n
                        dve.wait_ge(filled, base + u + 1)
                        last = nc.vector.reduce_max(part_max[:, j, c:c + 1], bank[:, 0:n], AX.X)
                    elif kind == "row":
                        dve.wait_ge(filled, base + u + 1)
                        last = nc.vector.tensor_copy(row_q[par][s.max_at:s.max_at + 1, a:a + n],
                                                     bank[s.max_at:s.max_at + 1, 0:n])
                    else:
                        dve.wait_ge(filled, base + u + 1)
                        g, j0 = len(a), a[0]
                        out = bank[:, 0:g * (D + 1)].rearrange("p (g n) -> p g n", n=D + 1)
                        nc.vector.reciprocal(inv[:, j0:j0 + g], out[:, :, D]).then_inc(inverted, 1)
                        dve.wait_ge(inverted, len(s.out_units) * h + i + 1)
                        for x, j in enumerate(a):
                            last = nc.vector.scalar_tensor_tensor(out=m.x[:, j, :], in0=out[:, x, 0:D],
                                                                  scalar=inv[:, j:j + 1], in1=m.x[:, j, :],
                                                                  op0=ALU.mult, op1=ALU.add)
                    last.then_inc(freed, 1)
                    if kind == "max" and s.last_chunk(j, c):
                        dve.wait_ge(freed, base + u + 1)
                        nc.vector.reduce_max(query_max[:, j:j + 1], part_max[:, j, 0:c + 1], AX.X).then_inc(max_done, 1)

                def prepare():
                    for u, unit in enumerate(s.prep_units):
                        take(unit, 0, u, 0, 0)

                def step(h, par, is_first, has_next):
                    base = unit_base(h)
                    for slot in step_units(is_first, has_next):
                        for u, unit in slot:
                            if unit[0] == "out":
                                take(unit, base, u, 1 - par, h - 1)
                            else:
                                take(unit, base, u, 1 - par, h + 1)

                def finish():
                    base = unit_base(H - 1) + first_out
                    for u, unit in enumerate(s.out_units):
                        take(unit, base, u, 1, H - 1)
                    dve.wait_ge(freed, base + first_out)

                run(dve, prepare, step, finish)


def add_row(m, tag, pieces, plain):
    nc = m.nc
    (spread, s0), (made, m0) = m.shared("row_spread", len(pieces) + 1), m.shared("row_made", 1)
    added, a0 = m.shared("row_added", QT)
    with ExitStack() as ctx:
        cols = m.sb(f"{tag}_cols", [P, max(1, len(pieces)), P], ctx=ctx)
        with nc.Block() as block:

            @block.tensor
            def _(pe):
                pe.wait_ge(spread, s0 + len(pieces) + 1)
                for i, (v, w) in enumerate(pieces):
                    nc.tensor.matmul(m.work[0][:, 0:D], cols[0:v.shape[0], i, :], w, start=(i == 0), stop=False)
                nc.tensor.matmul(m.work[0][:, 0:D], m.ones[0:1, :], plain, start=(not pieces),
                                 stop=True).then_inc(made, 1)

            @block.vector
            def _(dve):
                nc.vector.nop().then_inc(spread, 1)
                for i, (v, w) in enumerate(pieces):
                    nc.vector.tensor_scalar(cols[0:v.shape[0], i, :], m.ones[0:v.shape[0], :], v, None,
                                            ALU.mult).then_inc(spread, 1)
                dve.wait_ge(made, m0 + 1)
                for j in range(QT):
                    nc.vector.tensor_tensor(m.x[:, j, :], m.work[0][:, 0:D], m.x[:, j, :],
                                            ALU.add).then_inc(added, 1)
                dve.wait_ge(added, a0 + QT)


def feed_forward(m, w):
    nc = m.nc
    HID = 4
    with ExitStack() as ctx:
        sb = lambda name, shape, dt=F32: m.sb(name, shape, dt, ctx)
        w1, w2 = sb("f_w1", [D, HID * P]), sb("f_w2", [P, HID, D])
        b1, b2 = sb("f_b1", [P, HID]), sb("f_b2", [P, D])
        hid = sb("f_hid", [P, HID, NQ])
        load_columns(m, "f_in", [(w1[:, :], w["w1"]), (w2[:, :, :], w["w2"].rearrange("(c p) n -> p c n", p=P)),
                                 (b1[:, :], w["b1"].rearrange("(c p) -> p c", p=P)),
                                 (b2[:, :], row(w["b2"]).broadcast_to([P, D]))])
        up, gelu, down, taken = (m.sem(f"f_{s}") for s in ("up", "gelu", "down", "taken"))
        with nc.Block() as block:

            @block.tensor
            def _(pe):
                for c in range(HID):
                    for h in range(2):
                        n = 2 * c + h
                        if n >= 2:
                            pe.wait_ge(gelu, n - 1)
                        nc.tensor.matmul(m.work[n % 2][:, :], w1[:, c * P:(c + 1) * P],
                                         m.x_t[:, h * HALF:(h + 1) * HALF], start=True, stop=True).then_inc(up, 1)
                pe.wait_ge(gelu, 2 * HID)
                for j in range(QT):
                    if j >= 2:
                        pe.wait_ge(taken, 2 * (j - 1))
                    for c in range(HID):
                        last = nc.tensor.matmul(m.sums[j % 2][:, 0:D], hid[:, c, j * P:(j + 1) * P], w2[:, c, :],
                                                start=(c == 0), stop=(c == HID - 1))
                    last.then_inc(down, 1)

            @block.scalar
            def _(act):
                for n in range(2 * HID):
                    c, h = divmod(n, 2)
                    act.wait_ge(up, n + 1)
                    nc.scalar.activation(hid[:, c, h * HALF:(h + 1) * HALF], m.work[n % 2][:, :], ACT.Gelu,
                                         bias=b1[:, c:c + 1]).then_inc(gelu, 1)

            @block.vector
            def _(dve):
                for j in range(QT):
                    dve.wait_ge(down, j + 1)
                    nc.vector.tensor_tensor(m.x[:, j, :], m.sums[j % 2][:, 0:D], m.x[:, j, :],
                                            ALU.add).then_inc(taken, 1)
                    dve.wait_ge(taken, 2 * j + 1)
                    nc.vector.tensor_tensor(m.x[:, j, :], m.x[:, j, :], b2[:, :], ALU.add).then_inc(taken, 1)
                dve.wait_ge(taken, 2 * QT)


def copy_x(m, tag, dst):
    nc = m.nc
    done = m.sem(f"{tag}_done")
    with nc.Block() as block:

        @block.vector
        def _(dve):
            nc.vector.tensor_copy(dst[:, :, :], m.x[:, :, :]).then_inc(done, 1)
            dve.wait_ge(done, 1)


def normalized_queries(m, tag, gain, shift):
    with ExitStack() as ctx:
        rows = m.sb(f"{tag}_rows", [P, QT, D], ctx=ctx)
        cols = m.sb(f"{tag}_gs", [D, 2], ctx=ctx)
        load_columns(m, f"{tag}_gs", [(cols[:, 0:1], column(gain)), (cols[:, 1:2], column(shift))])
        normalize(m, f"{tag}_n", m.x, NQ, rows)
        turn(m, f"{tag}_t", rows, m.x_t, NQ, cols[:, 0:1], cols[:, 1:2])


def scan_layer(m, w, out):
    nc = m.nc
    S = 64
    BLK = 64
    with ExitStack() as ctx:
        sb = lambda name, shape, dt=F32: m.sb(name, shape, dt, ctx)
        w_in, w_in_t, bmat = sb("s_w_in", [D, D]), sb("s_w_in_t", [D, D]), sb("s_bmat", [D, S])
        a_nat, a_t = sb("s_a", [S, S]), sb("s_a_t", [P, S])
        cmat, b_in = sb("s_cmat", [S, D]), sb("s_b_in", [D, 1])
        y_t, u_t = sb("s_y_t", [D, NQ]), sb("s_u_t", [S, NQ])
        h_t = sb("s_h_t", [S, NQ + 1])
        h_blk = sb("s_h_blk", [P, BLK + 1])
        au_t = sb("s_au_t", [S, NQ])
        au_blk = sb("s_au_blk", [S, BLK])
        load_columns(m, "s_in", [(w_in[:, :], w["W_in"]), (bmat[:, :], w["Bmat"]), (a_nat[:, :], w["A"]),
                                 (cmat[:, :], w["Cmat"]), (b_in[:, :], column(w["b_in"]))])
        made, taken = m.sem("s_made"), m.sem("s_taken")
        with nc.Block() as block:

            @block.tensor
            def _(pe):
                nc.tensor.transpose(m.work[0][:, 0:D], w_in[:, :], m.ident[:, :]).then_inc(made, 1)
                nc.tensor.transpose(m.work[1][0:S, 0:S], a_nat[:, :], m.ident[0:S, 0:S]).then_inc(made, 1)
                pe.wait_ge(taken, 4)
                for h in range(2):
                    nc.tensor.matmul(m.work[h][:, :], w_in_t[:, :], m.x_t[:, h * HALF:(h + 1) * HALF], start=True,
                                     stop=True).then_inc(made, 1)
                for h in range(2):
                    pe.wait_ge(taken, 5 + h)
                    nc.tensor.matmul(m.sums[h][0:S, :], bmat[:, :], y_t[:, h * HALF:(h + 1) * HALF], start=True,
                                     stop=True).then_inc(made, 1)
                for h in range(2):
                    pe.wait_ge(taken, 7 + h)
                    nc.tensor.matmul(m.work[h][0:S, :], a_t[0:S, :], u_t[:, h * HALF:(h + 1) * HALF], start=True,
                                     stop=True).then_inc(made, 1)

            @block.vector
            def _(dve):
                nc.vector.memset(a_t[:, :], 0.0).then_inc(taken, 1)
                nc.vector.memset(h_blk[:, :], 0.0).then_inc(taken, 1)
                dve.wait_ge(made, 1)
                nc.vector.tensor_copy(w_in_t[:, :], m.work[0][:, 0:D]).then_inc(taken, 1)
                dve.wait_ge(made, 2)
                dve.wait_ge(taken, 2)
                nc.vector.tensor_copy(a_t[0:S, :], m.work[1][0:S, 0:S]).then_inc(taken, 1)
                for h in range(2):
                    dve.wait_ge(made, 3 + h)
                    nc.vector.tensor_scalar(y_t[:, h * HALF:(h + 1) * HALF], m.work[h][:, :], b_in[:, :], None,
                                            ALU.add).then_inc(taken, 1)
                for h in range(2):
                    dve.wait_ge(made, 5 + h)
                    nc.vector.tensor_copy(u_t[:, h * HALF:(h + 1) * HALF], m.sums[h][0:S, :]).then_inc(taken, 1)
                for h in range(2):
                    dve.wait_ge(made, 7 + h)
                    nc.vector.tensor_copy(au_t[:, h * HALF:(h + 1) * HALF],
                                          m.work[h][0:S, :]).then_inc(taken, 1)
                dve.wait_ge(taken, 10)

        summed, silu_done, u_ready, h_saved = (m.sem(f"s_{n}") for n in ("summed", "silu", "u_ready", "h_saved"))
        with nc.Block() as block:

            @block.tensor
            def _(pe):
                with pe.Fori(0, NQ // BLK) as b:
                    pe.wait_ge(u_ready, b + 1)
                    for i in range(BLK):
                        z = m.work[i % 2][0:S, 0:1]
                        if i >= 1:
                            pe.wait_ge(silu_done, b * BLK + i)
                        nc.tensor.matmul(z, a_t[:, :], h_blk[:, i:i + 1], start=True, stop=True).then_inc(summed, 1)

            @block.scalar
            def _(act):
                with act.Fori(0, NQ // BLK) as b:
                    act.wait_ge(u_ready, b + 1)
                    for i in range(BLK):
                        act.wait_ge(summed, b * BLK + i + 1)
                        nc.scalar.activation(h_blk[0:S, i + 1:i + 2], m.work[i % 2][0:S, 0:1], ACT.Silu,
                                             bias=au_blk[:, i:i + 1]).then_inc(silu_done, 1)

            @block.vector
            def _(dve):
                with dve.Fori(0, NQ // BLK) as b:
                    nc.vector.tensor_copy(au_blk[:, :], au_t[:, bass.ds(b * BLK, BLK)]).then_inc(u_ready, 1)
                    dve.wait_ge(silu_done, (b + 1) * BLK)
                    nc.vector.tensor_copy(h_t[:, bass.ds(b * BLK, BLK + 1)], h_blk[0:S, :]).then_inc(h_saved, 1)
                    dve.wait_ge(h_saved, 2 * b + 1)
                    nc.vector.tensor_copy(h_blk[0:S, 0:1], h_blk[0:S, BLK:BLK + 1]).then_inc(h_saved, 1)
                    dve.wait_ge(h_saved, 2 * b + 2)

        summed_s, put, added, stored = (m.sem(f"s_{n}") for n in ("states", "put", "added", "stored"))
        with nc.Block() as block:

            @block.vector
            def _(dve):
                nc.vector.tensor_tensor(h_t[:, 0:NQ], h_t[:, 0:NQ], u_t[:, :], ALU.add).then_inc(summed_s, 1)
                for j in range(QT):
                    dve.wait_ge(put, j + 1)
                    nc.vector.tensor_tensor(m.x[:, j, :], m.work[j % 2][:, 0:D], m.x[:, j, :],
                                            ALU.add).then_inc(added, 1)

            @block.tensor
            def _(pe):
                pe.wait_ge(summed_s, 1)
                for j in range(QT):
                    if j >= 2:
                        pe.wait_ge(added, j - 1)
                    nc.tensor.matmul(m.work[j % 2][:, 0:D], h_t[:, j * P:(j + 1) * P], cmat[:, :], start=True,
                                     stop=True).then_inc(put, 1)

            @block.sync
            def _(sp):
                sp.wait_ge(added, QT)
                sp.dma_start(out.rearrange("(t p) d -> p t d", p=P), m.x[:, :, :]).then_inc(stored, 16)
                sp.wait_ge(stored, 16)


def program(nc, A, out):
    with ExitStack() as ctx:
        m = Machine(nc, ctx)
        L = [{k[9:]: v for k, v in A.items() if k.startswith(f"L{i}_xattn_")} for i in range(4)]
        x_in = A["x"].rearrange("a s d -> (a s) d")
        ctx_in = A["ctx_1024"].rearrange("a s d -> (a s) d")
        prog_in = A["ctxb_2048x64"].rearrange("a s d -> (a s) d")
        constants(m)
        turn(m, "x_in", m.x, m.x_t, NQ, dram=x_in)
        with ExitStack() as c:
            rows = m.sb("ctx_rows", [P, KT, D], ctx=c)
            turn(m, "ctx_in", rows, m.ctx_t, NK, dram=ctx_in)

        gated_attention(m, dict(L[0], mask=A["mask_BxS_ff1"]), None)

        w1 = L[1]
        with ExitStack() as c:
            masks = {n: m.sb(f"mask_{n}", [P, P], ctx=c) for n in ("later_key", "earlier_query", "all")}
            masked = m.sem("masks_made")
            with nc.Block() as block:

                @block.gpsimd
                def _(pool):
                    for t in masks.values():
                        nc.gpsimd.memset(t[:, :], MASKED).then_inc(masked, 1)
                    pool.wait_ge(masked, 3)
                    nc.gpsimd.affine_select(out=masks["later_key"][:, :], in_=masks["later_key"][:, :],
                                            compare_op=ALU.is_gt, fill=0.0, base=0, pattern=[[1, P]],
                                            channel_multiplier=-1).then_inc(masked, 1)
                    nc.gpsimd.affine_select(out=masks["earlier_query"][:, :], in_=masks["earlier_query"][:, :],
                                            compare_op=ALU.is_gt, fill=0.0, base=0, pattern=[[-1, P]],
                                            channel_multiplier=1).then_inc(masked, 1)
                    pool.wait_ge(masked, 5)

            normalized_queries(m, "ln1", w1["ln1_g"], w1["ln1_b"])
            plain = m.sb("b_self", [1, D], ctx=c)
            load_columns(m, "b_self", [(plain[:, :], row(w1["proj_s_b"]))])
            add_row(m, "add_self", [], plain[:, :])
            head_attention(m, Heads("self", 16, 8, NQ, float(D) ** -0.5, causal=True),
                           dict(Wq=w1["Wq_s"], Wk=w1["Wk_s"], Wv=w1["Wv_s"], Wo=w1["proj_s_w"], bq=None),
                           m.x_t, m.x_t, masks)
        normalized_queries(m, "ln2", w1["ln2_g"], w1["ln2_b"])
        with ExitStack() as c:
            plain = m.sb("b_cross", [1, D], ctx=c)
            load_columns(m, "b_cross", [(plain[:, :], row(w1["proj_c_b"]))])
            add_row(m, "add_cross", [], plain[:, :])
        head_attention(m, Heads("cross", 16, 8, NK, float(D) ** -0.5),
                       dict(Wq=w1["Wq_c"], Wk=w1["Wk_c"], Wv=w1["Wv_c"], Wo=w1["proj_c_w"], bq=None),
                       m.ctx_t, m.x_t)
        normalized_queries(m, "ln3", w1["ln3_g"], w1["ln3_b"])
        feed_forward(m, w1)

        w2 = L[2]
        turn(m, "x2", m.x, m.x_t, NQ)
        with ExitStack() as c:
            wo = m.sb("wo2", [P, 8, D], ctx=c)
            bv = m.sb("bv2", [P, 8], ctx=c)
            bo = m.sb("bo2", [1, D], ctx=c)
            load_columns(m, "wo2", [(wo[:, :, :], w2["Wo"].rearrange("(c p) n -> p c n", p=P)),
                                    (bv[:, :], w2["bv"].rearrange("(c p) -> p c", p=P)), (bo[:, :], row(w2["bo"]))])
            add_row(m, "add2", [(bv[:, i:i + 1], wo[:, i, :]) for i in range(8)], bo[:, :])
        head_attention(m, Heads("wide", 16, 64, NK, 0.125, masked=True), w2, m.ctx_t, m.x_t, A["mask_BxS2_ik0"])
        normalize(m, "post2", m.x, NQ)
        with ExitStack() as c:
            gb = m.sb("gb2", [P, 2, D], ctx=c)
            load_columns(m, "gb2", [(gb[:, 0, :], row(w2["gamma"]).broadcast_to([P, D])),
                                    (gb[:, 1, :], row(w2["beta"]).broadcast_to([P, D]))])
            scaled = m.sem("post2_gained")
            with nc.Block() as block:

                @block.vector
                def _(dve):
                    for j in range(QT):
                        nc.vector.tensor_tensor(m.x[:, j, :], m.x[:, j, :], gb[:, 0, :], ALU.mult).then_inc(scaled, 1)
                    dve.wait_ge(scaled, QT)
                    for j in range(QT):
                        nc.vector.tensor_tensor(m.x[:, j, :], m.x[:, j, :], gb[:, 1, :], ALU.add).then_inc(scaled, 1)
                    dve.wait_ge(scaled, 2 * QT)

        w3 = L[3]
        with ExitStack() as c:
            rows = m.sb("ctx_rows3", [P, KT, D], ctx=c)
            gs = m.sb("gs3", [D, 2], ctx=c)
            loaded = m.sem("ctx3_in")
            with nc.Block() as block:

                @block.sync
                def _(sp):
                    done, count = load_rows(m, "ctx3", ctx_in, rows, NK, sp)
                    sp.dma_start(gs[:, 0:1], column(w3["g1"])).then_inc(loaded, 16)
                    sp.dma_start(gs[:, 1:2], column(w3["beta1"])).then_inc(loaded, 16)
                    sp.wait_ge(done, count)
                    sp.wait_ge(loaded, 32)

            normalize(m, "ctx3n", rows, NK)
            turn(m, "ctx3t", rows, m.ctx_t, NK, gs[:, 0:1], gs[:, 1:2])
        with ExitStack() as c:
            qkv = m.sb("qkv3", [P, 4, D], ctx=c)
            qkv_t = m.sb("qkv3_t", [D, 4 * P], ctx=c)
            load_columns(m, "qkv3", [(qkv[:, 0:3, :], w3["W_qkv"].rearrange("(c p) n -> p c n", p=P)),
                                     (qkv[:, 3, :], w3["W_o"])])
            turn(m, "qkv3t", qkv, qkv_t, 4 * P)
            w_t = nc.dram_tensor("layer3_weights_t", [D, 4 * P], F32, kind="Internal").ap()
            load_columns(m, "qkv3_out", [(w_t, qkv_t[:, :])])
            bv, bo = m.sb("bv3", [P, 1], ctx=c), m.sb("bo3", [1, D], ctx=c)
            load_columns(m, "b3", [(bv[:, :], column(w3["b_qkv"][2 * D:3 * D])), (bo[:, :], row(w3["b_o"]))])
            normalized_queries(m, "ln4", w3["g1"], w3["beta1"])
            add_row(m, "add3", [(bv[:, :], qkv_t[:, 3 * D:4 * D])], bo[:, :])
        head_attention(m, Heads("last", 8, 16, NK, 0.25),
                       dict(Wq=w_t[:, 0:D], Wk=w_t[:, D:2 * D], Wv=w_t[:, 2 * D:3 * D], Wo=w_t[:, 3 * D:4 * D],
                            bq=w3["b_qkv"][0:D], bk=w3["b_qkv"][D:2 * D]), m.ctx_t, m.x_t)
        normalized_queries(m, "ln5", w3["g2"], w3["beta2"])
        with ExitStack() as c:
            prog = m.sb("prog", [P, KT, 64], ctx=c)
            w_prog, w_prog_t = m.sb("w_prog", [P, 64], ctx=c), m.sb("w_prog_t", [64, D], ctx=c)
            mean, b_prog = m.sb("prog_mean", [64, 1], ctx=c), m.sb("b_prog", [1, D], ctx=c)
            load_columns(m, "prog", [(prog[:, 0:FULL, :], prog_in[0:FULL * P, :].rearrange("(t p) d -> p t d", p=P)),
                                     (prog[0:TAIL, FULL, :], prog_in[FULL * P:NK, :]),
                                     (w_prog[:, :], w3["W_prog"]), (b_prog[:, :], row(w3["b_prog"]))])
            made, copied = m.sem("prog_made"), m.sem("prog_copied")
            with nc.Block() as block:

                @block.tensor
                def _(pe):
                    for t in range(KT):
                        r = P if t < FULL else TAIL
                        last = nc.tensor.matmul(m.work[0][0:64, 0:1], prog[0:r, t, :], m.ones[0:r, 0:1],
                                                start=(t == 0), stop=(t == KT - 1))
                    last.then_inc(made, 1)
                    nc.tensor.transpose(m.work[1][0:64, 0:D], w_prog[:, :], m.ident[:, :]).then_inc(made, 1)

                @block.vector
                def _(dve):
                    dve.wait_ge(made, 2)
                    nc.vector.tensor_scalar(mean[:, :], m.work[0][0:64, 0:1], 1.0 / NK, None, ALU.mult).then_inc(copied, 1)
                    nc.vector.tensor_copy(w_prog_t[:, :], m.work[1][0:64, 0:D]).then_inc(copied, 1)
                    dve.wait_ge(copied, 2)

            add_row(m, "add_prog", [(mean[:, :], w_prog_t[:, :])], b_prog[:, :])
        scan_layer(m, w3, out.rearrange("a s d -> (a s) d"))


_UNUSED = ("itok_BxS2_4_31999",)


def kernel(**inputs):
    import numpy as _np
    import concourse.bacc as _bacc
    from concourse import mybir as _mybir
    from concourse.bass_utils import run_bass_kernel_spmd as _run

    nc = _bacc.Bacc("TRN2", target_bir_lowering=False, num_devices=1)
    arrays, args = {}, {}
    for name, value in inputs.items():
        if name in _UNUSED:
            continue
        a = _np.ascontiguousarray(value)
        arrays[f"in_{name}"] = a
        args[name] = nc.dram_tensor(f"in_{name}", a.shape, _mybir.dt.from_np(a.dtype), kind="ExternalInput").ap()
    out = nc.dram_tensor("out", (1, NQ, D), F32, kind="ExternalOutput").ap()
    program(nc, args, out)
    r = _run(nc, [arrays], core_ids=[0])
    return r.results[0]["out"]
```

```python
from contextlib import ExitStack

import concourse.bass as bass
from concourse import mybir

F32 = mybir.dt.float32
F32R = mybir.dt.float32r
I32 = mybir.dt.int32
ACT = mybir.ActivationFunctionType
ALU = mybir.AluOpType
AX = mybir.AxisListType

P = 128
D = 128
NQ = 1024
QT = NQ // P
HALF = NQ // 2
NK = 6404
KT = -(-NK // P)
KPAD = KT * P
FULL = NK // P
TAIL = NK - FULL * P
CHUNK = 512
EPS = 1e-5
MASKED = -1e20
NEVER = -1e30


def chunks(n, size=CHUNK):
    return [(a, min(size, n - a)) for a in range(0, n, size)]


class Machine:

    def __init__(self, nc, ctx):
        self.nc, self.ctx, self.counts = nc, ctx, {}
        self.scores = [self.psum(f"scores{i}", [P, NQ]) for i in range(2)]
        self.work = [self.psum(f"work{i}", [P, CHUNK]) for i in range(2)]
        self.sums = [self.psum(f"sums{i}", [P, CHUNK]) for i in range(2)]
        self.x = self.sb("x", [P, QT, D])
        self.x_t = self.sb("x_t", [D, NQ])
        self.ctx_t = self.sb("ctx_t", [D, NK])
        self.ident = self.sb("ident", [P, P])
        self.neg_ident = self.sb("neg_ident", [P, P])
        self.ones = self.sb("ones", [P, P])

    def sb(self, name, shape, dt=F32, ctx=None):
        return (ctx or self.ctx).enter_context(self.nc.sbuf_tensor(name, shape, dt))

    def psum(self, name, shape):
        return self.ctx.enter_context(self.nc.psum_tensor(name, shape, F32))

    def sem(self, name):
        return self.ctx.enter_context(self.nc.semaphore(name))

    def shared(self, name, total):
        if name not in self.counts:
            self.counts[name] = [self.sem(name), 0]
        sem, before = self.counts[name]
        self.counts[name][1] += total
        return sem, before


def constants(m):
    nc = m.nc
    made = m.sem("constants_made")
    with nc.Block() as block:

        @block.gpsimd
        def _(pool):
            nc.gpsimd.memset(m.ident[:, :], 0.0).then_inc(made, 1)
            nc.gpsimd.memset(m.neg_ident[:, :], 0.0).then_inc(made, 1)
            nc.gpsimd.memset(m.ones[:, :], 1.0).then_inc(made, 1)
            pool.wait_ge(made, 3)
            for tile, value in ((m.ident, 1.0), (m.neg_ident, -1.0)):
                nc.gpsimd.affine_select(out=tile[:, :], in_=tile[:, :], compare_op=ALU.not_equal, fill=value,
                                        base=0, pattern=[[-1, P]], channel_multiplier=1).then_inc(made, 1)
            pool.wait_ge(made, 5)


def load_rows(m, tag, dram, rows, n, queue):
    full = n // P
    total = 16 * (len(chunks(full, 13)) + (n > full * P))
    loaded, count = m.shared("rows_loaded", total)
    for a, w in chunks(full, 13):
        queue.dma_start(rows[:, a:a + w, :],
                        dram[a * P:(a + w) * P, :].rearrange("(t p) d -> p t d", p=P)).then_inc(loaded, 16)
        count += 16
    if n > full * P:
        queue.dma_start(rows[0:n - full * P, full, :], dram[full * P:n, :]).then_inc(loaded, 16)
        count += 16
    return loaded, count


def turn(m, tag, rows, out_t, n, gain=None, shift=None, dram=None):
    nc = m.nc
    parts = chunks(n)
    turned, t0 = m.shared("turned", len(parts))
    copied, c0 = m.shared("turn_copied", len(parts))
    landed, l0 = m.shared("turn_landed", 1)
    with nc.Block() as block:

        @block.sync
        def _(sp):
            if dram is not None:
                loaded, count = load_rows(m, tag, dram, rows, n, sp)
                sp.wait_ge(loaded, count)
            sp.nop().then_inc(landed, 1)

        @block.tensor
        def _(pe):
            pe.wait_ge(landed, l0 + 1)
            for i, (a, w) in enumerate(parts):
                if i >= 2:
                    pe.wait_ge(copied, c0 + i - 1)
                for b, r in chunks(w, P):
                    last = nc.tensor.transpose(m.work[i % 2][:, b:b + r], rows[0:r, (a + b) // P, :],
                                               m.ident[0:r, 0:r])
                last.then_inc(turned, 1)

        @block.vector
        def _(dve):
            for i, (a, w) in enumerate(parts):
                dve.wait_ge(turned, t0 + i + 1)
                if gain is None:
                    nc.vector.tensor_copy(out_t[:, a:a + w], m.work[i % 2][:, 0:w]).then_inc(copied, 1)
                else:
                    nc.vector.tensor_scalar(out_t[:, a:a + w], m.work[i % 2][:, 0:w], gain, shift,
                                            ALU.mult, ALU.add).then_inc(copied, 1)
            dve.wait_ge(copied, c0 + len(parts))


def normalize(m, tag, rows, n, out=None):
    nc = m.nc
    out = rows if out is None else out
    tiles = -(-n // P)
    widths = [min(P, n - t * P) for t in range(tiles)]
    (got, g0), (rooted, r0) = m.shared("stats", 2 + 2 * tiles), m.shared("stats_rooted", 1)
    (inverted, i0), (scaled, s0) = m.shared("stats_inverted", 1), m.shared("rows_scaled", tiles)
    with ExitStack() as ctx:
        stats = m.sb(f"{tag}_stats_sb", [P, tiles, 6], ctx=ctx)
        mean_var = m.sb(f"{tag}_mean_var", [P, tiles, 2], ctx=ctx)
        root = m.sb(f"{tag}_root", [P, tiles], ctx=ctx)
        inverse = m.sb(f"{tag}_inverse", [P, tiles], ctx=ctx)
        eps = m.sb(f"{tag}_eps", [P, 1], ctx=ctx)
        with nc.Block() as block:

            @block.vector
            def _(dve):
                nc.vector.memset(eps[:, :], EPS).then_inc(got, 1)
                nc.vector.memset(mean_var[:, :, :], 1.0).then_inc(got, 1)
                for t, r in enumerate(widths):
                    nc.vector.bn_stats(stats[0:r, t, :], rows[0:r, t, :]).then_inc(got, 1)
                dve.wait_ge(got, g0 + 2 + tiles)
                for t, r in enumerate(widths):
                    nc.vector.bn_aggr(mean_var[0:r, t, :], stats[0:r, t, :]).then_inc(got, 1)
                dve.wait_ge(rooted, r0 + 1)
                nc.vector.reciprocal(inverse[:, :], root[:, :]).then_inc(inverted, 1)
                dve.wait_ge(inverted, i0 + 1)
                for t, r in enumerate(widths):
                    nc.vector.tensor_scalar(out[0:r, t, :], rows[0:r, t, :], mean_var[0:r, t, 0:1],
                                            inverse[0:r, t:t + 1], ALU.subtract, ALU.mult).then_inc(scaled, 1)
                dve.wait_ge(scaled, s0 + tiles)

            @block.scalar
            def _(act):
                act.wait_ge(got, g0 + 2 + 2 * tiles)
                nc.scalar.activation(root[:, :], mean_var[:, :, 1], ACT.Sqrt, bias=eps[:, :]).then_inc(rooted, 1)
                act.wait_ge(rooted, r0 + 1)


def load_columns(m, tag, pairs):
    nc = m.nc
    loaded, before = m.shared("small_loaded", 16 * len(pairs))
    with nc.Block() as block:

        @block.sync
        def _(sp):
            for dst, src in pairs:
                sp.dma_start(dst, src, allow_slow_non_contiguous=True).then_inc(loaded, 16)
            sp.wait_ge(loaded, before + 16 * len(pairs))


def column(v):
    return v.rearrange("(p a) -> p a", a=1)


def row(v):
    return v.rearrange("(a n) -> a n", a=1)


def gated_attention(m, w, scratch_ctx):
    nc = m.nc
    scale = float(D) ** -0.5
    with ExitStack() as ctx:
        sb = lambda name, shape, dt=F32: m.sb(name, shape, dt, ctx)
        wq, wk, wv = (sb(f"g_w{n}", [D, D]) for n in "qkv")
        wg = sb("g_wg", [D, 2, D])
        bq, bk = sb("g_bq", [D, 1]), sb("g_bk", [D, 1])
        bv_row, bg_row = sb("g_bv_row", [P, D]), sb("g_bg_row", [P, D])
        mask = sb("g_mask", [P, QT])
        k_a, k_b = sb("g_k_a", [D, KPAD], F32R), sb("g_k_b", [D, KPAD], F32R)
        q_a, q_b = sb("g_q_a", [D, NQ], F32R), sb("g_q_b", [D, NQ], F32R)
        q_full = sb("g_q_full", [D, NQ])
        first_row = sb("g_first_row", [P, P], F32R)
        max_row = sb("g_max_row", [P, NQ], F32R)
        v = sb("g_v", [P, KT, D])
        probs = [sb(f"g_probs{i}", [P, NQ]) for i in range(3)]
        part_max = sb("g_part_max", [P, QT, 13])
        query_max = sb("g_query_max", [P, QT])
        load_columns(m, "g_in", [(wq[:, :], w["Wq"]), (wk[:, :], w["Wk"]), (wv[:, :], w["Wv"]),
                                 (wg[:, :, :], w["Wg"].rearrange("(a p) n -> p a n", a=2)),
                                 (bq[:, :], column(w["bq"])), (bk[:, :], column(w["bk"])),
                                 (bv_row[:, :], row(w["bv"]).broadcast_to([P, D])),
                                 (bg_row[:, :], row(w["bg"]).broadcast_to([P, D])),
                                 (mask[:, :], w["mask"].rearrange("a (t p) -> p (a t)", p=P))])
        k_parts, q_parts = chunks(NK), chunks(NQ)
        v_parts = chunks(KT, 4)
        nk, nq, nv = len(k_parts), len(q_parts), len(v_parts)
        n_max = QT * nk
        cleared, filled, rounded, freed, done = (m.sem(f"g_{s}") for s in
                                                 ("cleared", "filled", "rounded", "freed", "max_done"))
        with nc.Block() as block:

            @block.gpsimd
            def _(pool):
                nc.gpsimd.memset(k_a[:, NK:KPAD].bitcast(F32), 0.0).then_inc(cleared, 1)
                nc.gpsimd.memset(k_b[:, NK:KPAD].bitcast(F32), 0.0).then_inc(cleared, 1)
                nc.gpsimd.memset(first_row[:, :].bitcast(F32), 0.0).then_inc(cleared, 1)
                nc.gpsimd.memset(max_row[:, :].bitcast(F32), 0.0).then_inc(cleared, 1)
                pool.wait_ge(cleared, 4)
                nc.gpsimd.memset(first_row[0:1, :].bitcast(F32), 1.0).then_inc(cleared, 1)
                pool.wait_ge(cleared, 5)

            @block.tensor
            def _(pe):
                u = 0

                def bank():
                    if u >= 2:
                        pe.wait_ge(freed, u - 1)
                    return m.work[u % 2]

                for a, n in k_parts:
                    nc.tensor.matmul(bank()[:, 0:n], wk[:, :], m.ctx_t[:, a:a + n], start=True,
                                     stop=True).then_inc(filled, 1)
                    u += 1
                for a, n in q_parts:
                    nc.tensor.matmul(bank()[:, 0:n], wq[:, :], m.x_t[:, a:a + n], start=True,
                                     stop=True).then_inc(filled, 1)
                    u += 1
                for t0, n in v_parts:
                    out = bank()
                    for t in range(t0, t0 + n):
                        r = P if t < FULL else TAIL
                        last = nc.tensor.matmul(out[0:r, (t - t0) * D:(t - t0 + 1) * D],
                                                m.ctx_t[:, t * P:t * P + r], wv[:, :], start=True, stop=True)
                    last.then_inc(filled, 1)
                    u += 1
                for j in range(QT):
                    for a, n in k_parts:
                        nc.tensor.matmul(bank()[:, 0:n], q_a[:, j * P:(j + 1) * P], k_a[:, a:a + n],
                                         start=True, stop=True).then_inc(filled, 1)
                        u += 1
                pe.wait_ge(done, QT)
                for h, (a, n) in enumerate(q_parts):
                    out = bank()
                    for j in range(4):
                        last = nc.tensor.matmul(out[0:1, j * P:(j + 1) * P], query_max[:, 4 * h + j:4 * h + j + 1],
                                                m.neg_ident[:, :], start=True, stop=True)
                    last.then_inc(filled, 1)
                    u += 1

            @block.scalar
            def _(act):
                for i, (a, n) in enumerate(k_parts + q_parts):
                    act.wait_ge(filled, i + 1)
                    dst, bias = (k_a, bk) if i < nk else (q_a, bq)
                    nc.scalar.activation(dst[:, a:a + n], m.work[i % 2][:, 0:n], ACT.Identity,
                                         bias=bias[:, :]).then_inc(rounded, 1)

            @block.vector
            def _(dve):
                for i, (a, n) in enumerate(k_parts + q_parts):
                    dve.wait_ge(rounded, i + 1)
                    hi, lo, bias = (k_a, k_b, bk) if i < nk else (q_a, q_b, bq)
                    if i >= nk:
                        nc.vector.tensor_scalar(q_full[:, a:a + n], m.work[i % 2][:, 0:n], bias[:, :], None,
                                                ALU.add)
                    nc.vector.scalar_tensor_tensor(out=lo[:, a:a + n], in0=m.work[i % 2][:, 0:n],
                                                   scalar=bias[:, :], in1=hi[:, a:a + n].bitcast(F32),
                                                   op0=ALU.add, op1=ALU.subtract).then_inc(freed, 1)
                u = nk + nq
                for t0, n in v_parts:
                    dve.wait_ge(filled, u + 1)
                    whole = min(n, FULL - t0)
                    if whole:
                        last = nc.vector.tensor_copy(
                            v[:, t0:t0 + whole, :],
                            m.work[u % 2][:, 0:whole * D].rearrange("p (t d) -> p t d", d=D))
                    if whole < n:
                        last = nc.vector.tensor_copy(v[0:TAIL, FULL, :],
                                                     m.work[u % 2][0:TAIL, whole * D:(whole + 1) * D])
                    last.then_inc(freed, 1)
                    u += 1
                for j in range(QT):
                    for c, (a, n) in enumerate(k_parts):
                        dve.wait_ge(filled, u + 1)
                        nc.vector.reduce_max(part_max[:, j, c:c + 1], m.work[u % 2][:, 0:n], AX.X).then_inc(freed, 1)
                        u += 1
                    dve.wait_ge(freed, u)
                    nc.vector.reduce_max(query_max[:, j:j + 1], part_max[:, j, :], AX.X).then_inc(done, 1)
                dve.wait_ge(cleared, 5)
                for h, (a, n) in enumerate(q_parts):
                    dve.wait_ge(filled, u + 1)
                    nc.vector.tensor_copy(max_row[0:1, a:a + n], m.work[u % 2][0:1, 0:n]).then_inc(freed, 1)
                    u += 1
                dve.wait_ge(freed, u)

        scored, exped, added, out_copied = (m.sem(f"g_{s}") for s in ("scored", "exped", "added", "out_copied"))
        summed, folded = m.sem("g_summed"), m.sem("g_folded")
        den, sum_p = sb("g_den", [P, CHUNK]), sb("g_sum_p", [P, NQ])
        att_t = sb("g_att_t", [D, NQ])
        with nc.Block() as block:

            @block.tensor
            def _(pe):
                def score(t):
                    if t >= 2:
                        pe.wait_ge(exped, t - 1)
                    k = slice(t * P, (t + 1) * P)
                    for h in range(2):
                        out = m.scores[t % 2][:, h * HALF:(h + 1) * HALF]
                        q = slice(h * HALF, (h + 1) * HALF)
                        nc.tensor.matmul(out, k_a[:, k], q_a[:, q], start=True, stop=False)
                        nc.tensor.matmul(out, k_b[:, k], q_a[:, q], start=False, stop=False)
                        nc.tensor.matmul(out, k_a[:, k], q_b[:, q], start=False, stop=False)
                        last = nc.tensor.matmul(out, first_row[:, :], max_row[:, q], start=False, stop=True)
                    last.then_inc(scored, 1)

                def add(t):
                    pe.wait_ge(exped, t + 1)
                    r = P if t < FULL else TAIL
                    for h in range(2):
                        p = probs[t % 3][0:r, h * HALF:(h + 1) * HALF]
                        last = nc.tensor.matmul(m.sums[h][:, :], v[0:r, t, :], p, start=(t == 0), stop=(t == KT - 1))
                    last.then_inc(added, 1)

                for t in range(KT):
                    score(t)
                    if t >= 1:
                        add(t - 1)
                add(KT - 1)
                pe.wait_ge(summed, KT)
                for h in range(2):
                    nc.tensor.matmul(m.work[0][32 * h:32 * h + 32, :], m.ones[:, 0:32],
                                     sum_p[:, h * HALF:(h + 1) * HALF], start=True, stop=True).then_inc(folded, 1)

            @block.scalar
            def _(act):
                for t in range(KT):
                    act.wait_ge(scored, t + 1)
                    if t >= 3:
                        act.wait_ge(added, t - 2)
                        act.wait_ge(summed, t - 2)
                    r = P if t < FULL else TAIL
                    nc.scalar.activation(probs[t % 3][0:r, :], m.scores[t % 2][0:r, :], ACT.Exp,
                                         scale=scale).then_inc(exped, 1)

            @block.vector
            def _(dve):
                for t in range(KT):
                    dve.wait_ge(exped, t + 1)
                    r = P if t < FULL else TAIL
                    if t == 0:
                        nc.vector.tensor_copy(sum_p[:, :], probs[0][:, :]).then_inc(summed, 1)
                    else:
                        dve.wait_ge(summed, t)
                        nc.vector.tensor_tensor(sum_p[0:r, :], sum_p[0:r, :], probs[t % 3][0:r, :],
                                                ALU.add).then_inc(summed, 1)
                dve.wait_ge(added, KT)
                for h in range(2):
                    nc.vector.tensor_copy(att_t[:, h * HALF:(h + 1) * HALF], m.sums[h][:, :]).then_inc(out_copied, 1)
                dve.wait_ge(folded, 2)
                nc.vector.tensor_copy(den[0:64, :], m.work[0][0:64, :]).then_inc(out_copied, 1)
                dve.wait_ge(out_copied, 3)

        made, taken, link, gate_read, gate_exped = (m.sem(f"g_{s}") for s in
                                                    ("made", "taken", "link", "gate_read", "gate_exped"))
        att, gate, inv = sb("g_att", [P, QT, D]), sb("g_gate", [P, QT, D]), sb("g_inv", [P, QT])
        bias_made = m.sem("g_bias_made")
        bv_cols = sb("g_bv_cols", [P, P])
        bv_col = sb("g_bv_col", [P, 1])
        gate_bias = sb("g_gate_bias", [P, D])
        load_columns(m, "g_bv", [(bv_col[:, :], column(w["bv"]))])
        with nc.Block() as block:

            @block.tensor
            def _(pe):
                pe.wait_ge(bias_made, 1)
                nc.tensor.matmul(m.scores[0][:, 0:D], bv_cols[:, :], wg[:, 1, :], start=True,
                                 stop=True).then_inc(bias_made, 1)
                for j in range(QT):
                    if j >= 2:
                        pe.wait_ge(taken, j - 1)
                    q = slice(j * P, (j + 1) * P)
                    h, c = divmod(j, 4)
                    nc.tensor.transpose(m.work[j % 2][:, 0:D], att_t[:, q], m.ident[:, :])
                    nc.tensor.matmul(m.work[j % 2][:, D:2 * D], att_t[:, q], wg[:, 1, :], start=True, stop=True)
                    nc.tensor.matmul(m.work[j % 2][:, 2 * D:2 * D + 1], den[32 * h:32 * h + 1, c * P:(c + 1) * P],
                                     m.ones[32 * h:32 * h + 1, 0:1], start=True, stop=True)
                    nc.tensor.matmul(m.sums[j % 2][:, 0:D], q_full[:, q], wg[:, 0, :], start=True,
                                     stop=True).then_inc(made, 1)

            @block.vector
            def _(dve):
                count = [0]

                def chained(ins):
                    count[0] += 1
                    ins.then_inc(link, 1)
                    dve.wait_ge(link, count[0])

                nc.vector.tensor_scalar(bv_cols[:, :], m.ones[:, :], bv_col[:, :], None,
                                        ALU.mult).then_inc(bias_made, 1)
                dve.wait_ge(bias_made, 2)
                chained(nc.vector.tensor_tensor(gate_bias[:, :], m.scores[0][:, 0:D], bg_row[:, :], ALU.add))
                for j in range(QT):
                    dve.wait_ge(made, j + 1)
                    chained(nc.vector.reciprocal(inv[:, j:j + 1], m.work[j % 2][:, 2 * D:2 * D + 1]))
                    nc.vector.scalar_tensor_tensor(out=att[:, j, :], in0=m.work[j % 2][:, 0:D],
                                                   scalar=inv[:, j:j + 1], in1=bv_row[:, :],
                                                   op0=ALU.mult, op1=ALU.add)
                    chained(nc.vector.scalar_tensor_tensor(out=gate[:, j, :], in0=m.work[j % 2][:, D:2 * D],
                                                           scalar=inv[:, j:j + 1], in1=gate_bias[:, :],
                                                           op0=ALU.mult, op1=ALU.add))
                    nc.vector.tensor_tensor(gate[:, j, :], m.sums[j % 2][:, 0:D], gate[:, j, :],
                                            ALU.add).then_inc(taken, 1)
                dve.wait_ge(taken, QT)
                nc.vector.nop().then_inc(gate_read, 1)
                dve.wait_ge(gate_exped, 1)
                chained(nc.vector.tensor_scalar(gate[:, :, :], gate[:, :, :], 1.0, None, ALU.add))
                chained(nc.vector.reciprocal(gate[:, :, :], gate[:, :, :]))
                for j in range(QT):
                    last = nc.vector.tensor_scalar(att[:, j, :], att[:, j, :], mask[:, j:j + 1], None, ALU.mult)
                chained(last)
                chained(nc.vector.tensor_tensor(att[:, :, :], att[:, :, :], gate[:, :, :], ALU.mult))
                chained(nc.vector.tensor_tensor(m.x[:, :, :], att[:, :, :], m.x[:, :, :], ALU.add))

            @block.scalar
            def _(act):
                act.wait_ge(gate_read, 1)
                nc.scalar.activation(gate[:, :, :], gate[:, :, :], ACT.Exp, scale=-1.0).then_inc(gate_exped, 1)
                act.wait_ge(gate_exped, 1)


UNIT_COST = dict(out=1.5, k=2.5, q=2.5, max=1, row=1)


class Heads:

    def __init__(self, tag, heads, d, keys, scale, causal=False, masked=False):
        self.tag, self.heads, self.d, self.keys, self.scale = tag, heads, d, keys, scale
        self.causal, self.masked = causal, masked
        self.wide = d == 64
        self.blocks = [0, 64] if self.wide else [0, 32, 64]
        self.max_at = 64 if self.wide else 96
        self.tiles = -(-keys // P)
        self.k_parts, self.q_parts = chunks(keys), chunks(NQ)
        self.max_parts = [(j, c, a, n) for j in range(QT)
                          for c, (a, n) in enumerate(chunks((j + 1) * P if causal else keys))]
        self.n_probs = 2 if self.wide else 3
        self.out_units = [("out", c, list(range(a, a + n)), None) for c, (a, n) in enumerate(chunks(QT, 2))]
        prep = []
        if self.wide:
            prep += [("k", i, a, n) for i, (a, n) in enumerate(self.k_parts)]
            prep += [("q", i, a, n) for i, (a, n) in enumerate(self.q_parts)]
        self.n_split = len(self.k_parts) + len(self.q_parts)
        prep += [("max", j, c, (a, n)) for j, c, a, n in self.max_parts]
        prep += [("row", i, a, n) for i, (a, n) in enumerate(self.q_parts)]
        self.prep_units = prep

    def rows(self, t):
        return min(P, self.keys - t * P)

    def first_query(self, t):
        return P * t if self.causal and t >= 2 else 0

    def last_chunk(self, j, c):
        return c == max(cc for jj, cc, _, _ in self.max_parts if jj == j)


def all_values(m, tag, dram, wv, key_t, v_all, keys):
    nc = m.nc
    tiles, width = -(-keys // P), wv.shape[1]
    parts = chunks(tiles, CHUNK // width)
    made, taken, loaded = (m.sem(f"{tag}_v_{n}") for n in ("made", "taken", "loaded"))
    with nc.Block() as block:

        @block.sync
        def _(sp):
            sp.dma_start(wv[:, :], dram).then_inc(loaded, 16)

        @block.tensor
        def _(pe):
            pe.wait_ge(loaded, 16)
            for i, (a, n) in enumerate(parts):
                if i >= 2:
                    pe.wait_ge(taken, i)
                for t in range(a, a + n):
                    r = min(P, keys - t * P)
                    last = nc.tensor.matmul(m.work[i % 2][0:r, (t - a) * width:(t - a + 1) * width],
                                            key_t[:, t * P:t * P + r], wv[:, :], start=True, stop=True)
                last.then_inc(made, 1)

        @block.vector
        def _(dve):
            nc.vector.memset(v_all[:, tiles - 1, :], 0.0).then_inc(taken, 1)
            dve.wait_ge(taken, 1)
            for i, (a, n) in enumerate(parts):
                dve.wait_ge(made, i + 1)
                whole = min(n, keys // P - a)
                if whole:
                    last = nc.vector.tensor_copy(v_all[:, a:a + whole, :],
                                                 m.work[i % 2][:, 0:whole * width].rearrange("p (t w) -> p t w", w=width))
                if whole < n:
                    r = keys - (a + whole) * P
                    last = nc.vector.tensor_copy(v_all[0:r, a + whole, :],
                                                 m.work[i % 2][0:r, whole * width:(whole + 1) * width])
                last.then_inc(taken, 1)
            dve.wait_ge(taken, len(parts) + 1)


def stored_values(m, s, w, key_t):
    nc, tag, d, H = m.nc, s.tag, s.d, s.heads
    v_dram = nc.dram_tensor(f"{tag}_values", [H, P, s.tiles, d], F32, kind="Internal").ap()
    groups = chunks(s.tiles, 4)
    per_bank = CHUNK // d
    banks = [m.work, m.sums]
    with ExitStack() as ctx:
        wv = m.sb(f"{tag}_wv_all", [D, H * d], ctx=ctx)
        rows = [m.sb(f"{tag}_v_rows{i}", [P, H, 4, d], ctx=ctx) for i in range(2)]
        loaded, made = m.sem(f"{tag}_wv_loaded"), m.sem(f"{tag}_values_made")
        taken = [m.sem(f"{tag}_values_taken{i}") for i in range(2)]
        stored = [m.sem(f"{tag}_values_stored{i}") for i in range(2)]
        with nc.Block() as block:

            @block.sync
            def _(sp):
                sp.dma_start(wv[:, :], w["Wv"]).then_inc(loaded, 16)
                for g, (t0, n) in enumerate(groups):
                    r = s.rows(t0 + n - 1)
                    whole = n if r == P else n - 1
                    for half in range(2):
                        sp.wait_ge(taken[half], t0 + n)
                    if whole:
                        sp.dma_start(v_dram[:, :, t0:t0 + whole, :].rearrange("h p t e -> p h t e"),
                                     rows[g % 2][:, :, 0:whole, :]).then_inc(stored[g % 2], 16)
                    if whole < n:
                        sp.dma_start(v_dram[:, 0:r, t0 + whole, :].rearrange("h p e -> p h e"),
                                     rows[g % 2][0:r, :, whole, :]).then_inc(stored[g % 2], 16)
                ragged = len(groups) - 1 if whole and whole < n else None
                for i in range(2):
                    sp.wait_ge(stored[i], 16 * (len(range(i, len(groups), 2)) + (ragged is not None and ragged % 2 == i)))

            @block.tensor
            def _(pe):
                pe.wait_ge(loaded, 16)
                for t in range(s.tiles):
                    r = s.rows(t)
                    for half in range(2):
                        if t >= 2:
                            pe.wait_ge(taken[half], t - 1)
                        nc.tensor.matmul(banks[t % 2][half][0:r, :], key_t[:, t * P:t * P + r],
                                         wv[:, half * CHUNK:(half + 1) * CHUNK], start=True, stop=True).then_inc(made, 1)

            def take(engine, half):
                for t in range(s.tiles):
                    g, r = t // 4, s.rows(t)
                    engine.wait_ge(made, 2 * t + half + 1)
                    if t % 4 == 0 and g >= 2:
                        engine.wait_ge(stored[g % 2], 16 * (g // 2))
                    yield (rows[g % 2][0:r, half * per_bank:(half + 1) * per_bank, t % 4, :],
                           banks[t % 2][half][0:r, :].rearrange("p (h e) -> p h e", e=d))

            @block.scalar
            def _(act):
                for dst, src in take(act, 0):
                    nc.scalar.activation(dst, src, ACT.Copy).then_inc(taken[0], 1)

            @block.vector
            def _(dve):
                for dst, src in take(dve, 1):
                    nc.vector.tensor_copy(dst, src).then_inc(taken[1], 1)
    return v_dram


def split_projections(m, s, w, key_t, query_t):
    nc, tag = m.nc, s.tag
    k_dram = nc.dram_tensor(f"{tag}_k_parts", [2, P, s.keys], F32, kind="Internal").ap()
    q_dram = nc.dram_tensor(f"{tag}_q_parts", [2, P + 1, NQ], F32, kind="Internal").ap()
    jobs = [(0, a, n) for a, n in s.k_parts] + [(1, a, n) for a, n in s.q_parts]
    biased = w["bq"] is not None
    loads = 4 if biased else 2
    RING = 4
    with ExitStack() as ctx:
        hi = [m.sb(f"{tag}_hi{i}", [P, CHUNK], F32R, ctx) for i in range(RING)]
        lo = [m.sb(f"{tag}_lo{i}", [P, CHUNK], F32R, ctx) for i in range(RING)]
        weights = [m.sb(f"{tag}_w{n}_all", [D, P], ctx=ctx) for n in "kq"]
        bias = [m.sb(f"{tag}_b{n}_all", [P, 1], ctx=ctx) for n in "kq"]
        zeros = m.sb(f"{tag}_zeros", [1, NQ], ctx=ctx)
        loaded, i0 = m.shared("split_loaded", 16 * (loads + 1))
        cleared, z0 = m.shared("split_cleared", 3)
        made, m0 = m.shared("split_made", len(jobs))
        rounded, r0 = m.shared("split_rounded", len(jobs))
        parted, p0 = m.shared("split_parted", len(jobs))
        uses = [len(range(i, len(jobs), RING)) for i in range(RING)]
        stored = [m.shared(f"split_stored{i}", 32 * uses[i]) for i in range(RING)]
        with nc.Block() as block:

            @block.sync
            def _(sp):
                sp.wait_ge(cleared, z0 + 3)
                sp.dma_start(weights[0][:, :], w["Wk"]).then_inc(loaded, 16)
                sp.dma_start(weights[1][:, :], w["Wq"]).then_inc(loaded, 16)
                if biased:
                    sp.dma_start(bias[0][:, :], column(w["bk"])).then_inc(loaded, 16)
                    sp.dma_start(bias[1][:, :], column(w["bq"])).then_inc(loaded, 16)
                sp.dma_start(q_dram[0, P:P + 1, :], zeros[:, :]).then_inc(loaded, 16)
                for u, (which, a, n) in enumerate(jobs):
                    dst = (k_dram, q_dram)[which]
                    sp.wait_ge(parted, p0 + u + 1)
                    sp.dma_start(dst[0, 0:P, a:a + n], hi[u % RING][:, 0:n].bitcast(F32)).then_inc(stored[u % RING][0], 16)
                    sp.dma_start(dst[1, 0:P, a:a + n], lo[u % RING][:, 0:n].bitcast(F32)).then_inc(stored[u % RING][0], 16)
                for (done, before), n in zip(stored, uses):
                    sp.wait_ge(done, before + 32 * n)

            @block.gpsimd
            def _(pool):
                nc.gpsimd.memset(bias[0][:, :], 0.0).then_inc(cleared, 1)
                nc.gpsimd.memset(bias[1][:, :], 0.0).then_inc(cleared, 1)
                nc.gpsimd.memset(zeros[:, :], 0.0).then_inc(cleared, 1)

            @block.tensor
            def _(pe):
                pe.wait_ge(loaded, i0 + 16 * (loads + 1))
                for u, (which, a, n) in enumerate(jobs):
                    if u >= 2:
                        pe.wait_ge(parted, p0 + u - 1)
                    nc.tensor.matmul(m.work[u % 2][:, 0:n], weights[which][:, :],
                                     (key_t, query_t)[which][:, a:a + n], start=True, stop=True).then_inc(made, 1)

            @block.scalar
            def _(act):
                act.wait_ge(loaded, i0 + 16 * (loads + 1))
                for u, (which, a, n) in enumerate(jobs):
                    act.wait_ge(made, m0 + u + 1)
                    if u >= RING:
                        done, before = stored[u % RING]
                        act.wait_ge(done, before + 32 * (u // RING))
                    nc.scalar.activation(hi[u % RING][:, 0:n], m.work[u % 2][:, 0:n], ACT.Identity,
                                         bias=bias[which][:, :]).then_inc(rounded, 1)

            @block.vector
            def _(dve):
                for u, (which, a, n) in enumerate(jobs):
                    dve.wait_ge(rounded, r0 + u + 1)
                    nc.vector.scalar_tensor_tensor(out=lo[u % RING][:, 0:n], in0=m.work[u % 2][:, 0:n],
                                                   scalar=bias[which][:, :], in1=hi[u % RING][:, 0:n].bitcast(F32),
                                                   op0=ALU.add, op1=ALU.subtract).then_inc(parted, 1)
    return k_dram, q_dram


def head_attention(m, s, w, key_t, query_t, masks=None):
    nc, tag, d = m.nc, s.tag, s.d
    H, NT = s.heads, s.tiles
    if not s.wide:
        k_dram, q_dram = split_projections(m, s, w, key_t, query_t)
    else:
        v_dram = stored_values(m, s, w, key_t)
    with ExitStack() as ctx:
        sb = lambda name, shape, dt=F32: m.sb(f"{tag}_{name}", shape, dt, ctx)
        keys_w = NT * P
        k_s = [sb(f"k{i}", [P, keys_w], F32R) for i in range(2)]
        q_s = [sb(f"q{i}", [P, NQ], F32R) for i in range(2)]
        if s.wide:
            k2_s = [sb(f"k2{i}", [P, keys_w], F32R) for i in range(2)]
            q2_s = [sb(f"q2{i}", [P, NQ], F32R) for i in range(2)]
            qm_s = [sb(f"qm{i}", [P, NQ], F32R) for i in range(2)]
            passes = [(k_s, q_s), (k2_s, q2_s)]
            max_q, max_k, row_q = qm_s, k2_s, q2_s
            den_s = sb("den", [P, CHUNK])
            mask_int, mask_bias = sb("mask_int", [P, NT], I32), sb("mask_bias", [P, NT])
        else:
            passes = [(k_s, q_s)]
            max_q, max_k, row_q = q_s, k_s, q_s
        v_w = 64 if s.wide else 32
        v_s = [sb(f"v{i}", [P, NT, v_w]) for i in range(2)]
        probs = [sb(f"probs{i}", [P, NQ]) for i in range(s.n_probs)]
        if s.wide:
            wk_s, wq_s = ([sb(f"{n}{i}", [D, P]) for i in range(2)] for n in ("wk", "wq"))
            bk_s, bq_s = ([sb(f"{n}{i}", [P, 1]) for i in range(2)] for n in ("bk", "bq"))
            sum_p = sb("sum_p", [P, NQ])
            v_in, folded = [m.sem(f"{tag}_v_in{i}") for i in range(2)], m.sem(f"{tag}_folded")
            summed = [m.sem(f"{tag}_summed{i}") for i in range(2)]
        else:
            v_all, wv = sb("v_all", [P, NT, H * d]), sb("wv", [D, H * d])
        wo_s = [sb(f"wo{i}", [P, D + 1]) for i in range(2)]
        acc_s = sb("acc", [P, CHUNK])
        part_max = sb("part_max", [P, QT, 13])
        query_max = sb("query_max", [P, QT])
        inv = sb("inv", [P, QT])

        sem = lambda name: m.sem(f"{tag}_{name}")
        cleared, mask_in, mask_done = sem("cleared"), sem("mask_in"), sem("mask_done")
        mask_zero, keys_in = sem("mask_zero"), sem("keys_in")
        keys_zero, zero_before = m.shared("keys_zero", 2)
        staged, out_staged = ([sem(f"{n}staged{i}") for i in range(2)] for n in ("", "out_"))
        filled, rounded, freed = (sem(n) for n in ("filled", "rounded", "freed"))
        tile_max, max_done, inverted = sem("tile_max"), sem("max_done"), sem("inverted")
        scored, exped, added, acc_taken = (sem(n) for n in ("scored", "exped", "added", "acc_taken"))

        with nc.Block() as block:

            @block.gpsimd
            def _(pool):
                n = 0

                def put(value, ap):
                    nonlocal n
                    nc.gpsimd.memset(ap, value).then_inc(cleared, 1)
                    n += 1
                    pool.wait_ge(cleared, n)

                whole = s.keys // P
                if s.masked:
                    nc.gpsimd.memset(mask_int[:, :], 0).then_inc(mask_zero, 1)
                for i in range(2):
                    for t in (wo_s[i],) + ((wk_s[i], wq_s[i], bk_s[i], bq_s[i]) if s.wide else ()):
                        put(0.0, t[:, :])
                for i in range(2):
                    if s.wide:
                        if whole < NT:
                            put(0.0, k_s[i][:, s.keys:keys_w].bitcast(F32))
                            put(0.0, k2_s[i][0:64, s.keys:keys_w].bitcast(F32))
                        for t in (q2_s[i], qm_s[i]):
                            put(0.0, t[:, :].bitcast(F32))
                        for at in (0, 64):
                            put(1.0, wo_s[i][at:at + 1, D:D + 1])
                        put(1.0, k2_s[i][64:96, :].bitcast(F32))
                        put(1.0, qm_s[i][96:97, :].bitcast(F32))
                        if whole < NT:
                            put(0.0, v_s[i][:, whole, :])
                    else:
                        put(1.0, k_s[i][96:128, 0:s.keys].bitcast(F32))
                        if whole < NT:
                            put(0.0, k_s[i][96:128, s.keys:keys_w].bitcast(F32))
                        put(0.0, q_s[i][:, :].bitcast(F32))
                        put(0.0, v_s[i][:, :, :])
                        put(1.0, v_s[i][:, 0:whole, d:d + 1])
                        if whole < NT:
                            put(1.0, v_s[i][0:s.rows(whole), whole, d:d + 1])

            @block.vector
            def _(dve):
                for i in range(2):
                    zeros = k2_s[i][96:128, :] if s.wide else k_s[i][0:96, :]
                    nc.vector.memset(zeros.bitcast(F32), 0.0).then_inc(keys_zero, 1)
                dve.wait_ge(keys_zero, zero_before + 2)

            if not s.wide:

                @block.sync
                def _(sp):
                    sp.wait_ge(cleared, 2)
                    for i in range(2):
                        for at in (0, 32, 64, 96):
                            sp.dma_start(wo_s[i][at + d:at + d + 1, D:D + 1], m.ones[0:1, 0:1]).then_inc(mask_in, 16)
                    sp.wait_ge(mask_in, 16 * 8)

        if s.masked:
            with nc.Block() as block:

                @block.sync
                def _(sp):
                    whole = s.keys // P
                    sp.dma_start(mask_int[:, 0:whole], masks[0, 0:whole * P].rearrange("(t p) -> p t", p=P),
                                 allow_slow_non_contiguous=True).then_inc(keys_in, 16)
                    sp.dma_start(mask_int[0:s.rows(whole), whole:NT], column(masks[0, whole * P:s.keys]),
                                 allow_slow_non_contiguous=True).then_inc(keys_in, 16)
                    for i, (a, n) in enumerate(chunks(s.keys, NQ)):
                        if i >= 2:
                            sp.wait_ge(mask_done, i - 1)
                        sp.dma_start(probs[i % 2][96:97, 0:n].bitcast(I32), masks[:, a:a + n]).then_inc(mask_in, 16)
                        sp.wait_ge(mask_in, 16 * (i + 1))

                @block.vector
                def _(dve):
                    for i, (a, n) in enumerate(chunks(s.keys, NQ)):
                        dve.wait_ge(mask_in, 16 * (i + 1))
                        for b in range(2):
                            last = nc.vector.tensor_scalar(k2_s[b][96:97, a:a + n], probs[i % 2][96:97, 0:n].bitcast(I32),
                                                           0.0, MASKED, ALU.is_equal, ALU.mult)
                        last.then_inc(mask_done, 1)
                    dve.wait_ge(keys_in, 32)
                    nc.vector.tensor_scalar(mask_bias[:, :], mask_int[:, :], 0.0, NEVER, ALU.is_equal,
                                            ALU.mult).then_inc(mask_done, 1)
                    dve.wait_ge(mask_done, i + 2)

        if not s.wide:
            all_values(m, tag, w["Wv"], wv, key_t, v_all, s.keys)

        stacked = list(zip(s.blocks, (0, 0, 1), (0, 1, 0)))
        stage_dmas = 2 * len(s.blocks) + (0 if s.wide else 1)
        out_dmas = 2 if s.wide else 4
        if s.wide:
            stage_dmas += 2 * len(s.blocks)

        work = m.work + [m.sums[1]]
        NW = len(work)

        U = len(s.out_units) + len(s.prep_units)
        UP = len(s.prep_units)
        first_out = len(s.out_units)

        def unit_base(h):
            return UP if isinstance(h, int) and h == 0 else 2 * UP + (h - 1) * U

        def step_units(h_is_first, has_next):
            units = ([] if h_is_first else s.out_units) + (s.prep_units if has_next is not None else [])
            slots = [[] for _ in range(NT)]
            cost = [UNIT_COST[unit[0]] for unit in units]
            for u, unit in enumerate(units):
                slots[1 + int(sum(cost[:u]) * (NT - 2) / sum(cost))].append((u, unit))
            return slots

        def prev_user(t, ring):
            return t - ring if t >= ring else max(x for x in range(NT) if x % ring == t % ring) - NT

        def run(engine, prepare, step, finish):
            prepare()
            step(0, 0, True, 1)
            with engine.Fori(0, (H - 2) // 2) as i:
                step(2 * i + 1, 1, False, i + 2)
                step(2 * i + 2, 0, False, i + 2)
            step(H - 1, 1, False, None)
            finish()

        with nc.Block() as block:

            @block.sync
            def _(sp):
                def stage(h, par):
                    cols = bass.ds(h * d, d)
                    if not s.wide:
                        for at, k_part, q_part in stacked:
                            sp.dma_start(k_s[par][at:at + d, 0:s.keys].bitcast(F32),
                                         k_dram[k_part, cols, :]).then_inc(staged[par], 16)
                            sp.dma_start(q_s[par][at:at + d, :].bitcast(F32),
                                         q_dram[q_part, cols, :]).then_inc(staged[par], 16)
                        sp.dma_start(q_s[par][s.max_at:s.max_at + 1, :].bitcast(F32),
                                     q_dram[0, P:P + 1, :]).then_inc(staged[par], 16)
                        return
                    for at in s.blocks:
                        sp.dma_start(wk_s[par][:, at:at + d], w["Wk"][:, cols]).then_inc(staged[par], 16)
                        sp.dma_start(wq_s[par][:, at:at + d], w["Wq"][:, cols]).then_inc(staged[par], 16)
                        sp.dma_start(bk_s[par][at:at + d, :], column(w["bk"])[cols, :]).then_inc(staged[par], 16)
                        sp.dma_start(bq_s[par][at:at + d, :], column(w["bq"])[cols, :]).then_inc(staged[par], 16)

                def stage_out(h, par):
                    for at in ((0, 64) if s.wide else (0, 32, 64, 96)):
                        sp.dma_start(wo_s[par][at:at + d, 0:D],
                                     w["Wo"][bass.ds(h * d, d), :]).then_inc(out_staged[par], 16)

                def stage_values(h, par):
                    whole = s.keys // P
                    r = s.rows(whole)
                    sp.dma_start(v_s[par][:, 0:whole, :], v_dram[bass.ds(h, 1), :, 0:whole, :].rearrange(
                        "h p t e -> (h p) t e")).then_inc(v_in[par], 16)
                    sp.dma_start(v_s[par][0:r, whole, :], v_dram[bass.ds(h, 1), 0:r, whole, :].rearrange(
                        "h p e -> (h p) e")).then_inc(v_in[par], 16)

                stage(0, 0)
                stage(1, 1)
                if s.wide:
                    stage_values(0, 0)
                    stage_values(1, 1)
                stage_out(0, 0)
                stage_out(1, 1)
                if s.wide:
                    sp.wait_ge(freed, UP)
                    stage(2, 0)

                def step(h, par, more):
                    if s.wide and more:
                        sp.wait_ge(freed, unit_base(h))
                        stage(h + 2, par)
                    sp.wait_ge(added, h * NT)
                    if s.wide:
                        stage_values(h + 1, 1 - par)
                    else:
                        stage(h + 1, 1 - par)
                    sp.wait_ge(freed, unit_base(h) + first_out)
                    stage_out(h + 1, 1 - par)

                with sp.Fori(0, (H - 4) // 2) as i:
                    step(2 * i + 1, 1, True)
                    step(2 * i + 2, 0, True)
                step(H - 3, 1, True)
                step(H - 2, 0, False)
                for par in range(2):
                    sp.wait_ge(staged[par], 16 * stage_dmas * (H // 2))
                    sp.wait_ge(out_staged[par], 16 * out_dmas * (H // 2))
                    if s.wide:
                        sp.wait_ge(v_in[par], 32 * (H // 2))

            @block.tensor
            def _(pe):
                def fill(unit, base, u, par, h, nth=0):
                    kind, i, a, n = unit
                    bank = work[u % NW]
                    if u >= NW:
                        pe.wait_ge(freed, base + u - NW + 1)
                    if kind == "out":
                        if i == 0:
                            pe.wait_ge(out_staged[par], 16 * out_dmas * nth)
                            pe.wait_ge(acc_taken, h + 1)
                        for g, j in enumerate(a):
                            half, c = divmod(j, 4)
                            r = slice(64 * half, 64 * half + 64)
                            o = g * (D + 1)
                            if s.wide:
                                nc.tensor.matmul(bank[:, o:o + D], acc_s[r, c * P:(c + 1) * P], wo_s[par][r, 0:D],
                                                 start=True, stop=True)
                                last = nc.tensor.matmul(bank[:, o + D:o + D + 1], den_s[r, c * P:(c + 1) * P],
                                                        wo_s[par][r, D:D + 1], start=True, stop=True)
                            else:
                                last = nc.tensor.matmul(bank[:, o:o + D + 1], acc_s[r, c * P:(c + 1) * P],
                                                        wo_s[par][r, :], start=True, stop=True)
                    elif kind == "k":
                        if i == 0:
                            pe.wait_ge(staged[par], 16 * stage_dmas * nth)
                        last = nc.tensor.matmul(bank[:, 0:n], wk_s[par][:, :], key_t[:, a:a + n], start=True, stop=True)
                    elif kind == "q":
                        last = nc.tensor.matmul(bank[:, 0:n], wq_s[par][:, :], query_t[:, a:a + n], start=True, stop=True)
                    elif kind == "max":
                        j, c, (a, n) = i, a, n
                        if j == 0 and c == 0:
                            if s.wide:
                                pe.wait_ge(freed, base + u)
                            else:
                                pe.wait_ge(staged[par], 16 * stage_dmas * nth)
                        edge = s.causal and s.last_chunk(j, c)
                        last = nc.tensor.matmul(bank[:, 0:n], max_q[par][:, j * P:(j + 1) * P],
                                                max_k[par][:, a:a + n], start=True, stop=not edge)
                        if edge:
                            last = nc.tensor.matmul(bank[:, n - P:n], m.ident[:, :], masks["later_key"][:, :],
                                                    start=False, stop=True)
                    else:
                        if i == 0:
                            pe.wait_ge(max_done, QT * (h + 1))
                        for c in range(4):
                            j = 4 * i + c
                            last = nc.tensor.matmul(bank[s.max_at:s.max_at + 1, c * P:(c + 1) * P],
                                                    query_max[:, j:j + 1], m.neg_ident[:, :], start=True, stop=True)
                    last.then_inc(filled, 1)

                def score(h, par, t, half):
                    prev = prev_user(t, 2)
                    first = half == (1 if s.first_query(t) >= HALF else 0)
                    if first and not (isinstance(h, int) and h == 0 and prev < 0):
                        pe.wait_ge(exped, h * NT + prev + 1)
                    a, b = max(s.first_query(t), half * HALF), (half + 1) * HALF
                    if a >= b:
                        return
                    out = m.scores[t % 2][:, a:b]
                    diagonal = s.causal and half * HALF <= t * P < b
                    for n, (ks, qs) in enumerate(passes):
                        last = nc.tensor.matmul(out, ks[par][:, t * P:(t + 1) * P], qs[par][:, a:b],
                                                start=(n == 0), stop=(n == len(passes) - 1 and not diagonal))
                    if s.causal and t == 1 and half == 0:
                        nc.tensor.matmul(m.scores[t % 2][:, 0:P], m.ident[:, :], masks["all"][:, :],
                                         start=False, stop=False)
                    if diagonal:
                        last = nc.tensor.matmul(m.scores[t % 2][:, t * P:(t + 1) * P], m.ident[:, :],
                                                masks["earlier_query"][:, :], start=False, stop=True)
                    if half == 1:
                        last.then_inc(scored, 1)

                def add(h, par, t, part):
                    if part == 0:
                        pe.wait_ge(exped, h * NT + t + 1)
                        if t == 0 and not (isinstance(h, int) and h == 0):
                            pe.wait_ge(acc_taken, h)
                    half = part
                    a, b = max(s.first_query(t), half * HALF), (half + 1) * HALF
                    if a >= b:
                        return
                    p = probs[t % s.n_probs][:, a:b]
                    o = slice(a - half * HALF, b - half * HALF)
                    tiles = [x for x in range(NT) if s.first_query(x) < b]
                    ends = t in tiles[-2:]
                    if s.wide:
                        last = nc.tensor.matmul(m.sums[0][64 * half:64 * half + 64, o], v_s[par][:, t, :], p,
                                                start=(t == 0), stop=(t == NT - 1))
                    else:
                        at = 64 * half + 32 * (t % 2)
                        last = nc.tensor.matmul(m.sums[0][at:at + 32, o], v_s[par][:, t, :], p,
                                                start=(t < 2), stop=ends)
                    if part == 1:
                        last.then_inc(added, 1)

                def fold(h, units):
                    pe.wait_ge(freed, units)
                    for half in range(2):
                        pe.wait_ge(summed[half], (h + 1) * NT)
                        nc.tensor.matmul(m.sums[1][64 * half:64 * half + 64, :], m.ones[:, 0:64],
                                         sum_p[:, half * HALF:(half + 1) * HALF], start=True,
                                         stop=True).then_inc(folded, 1)

                def prepare():
                    for u, unit in enumerate(s.prep_units):
                        fill(unit, 0, u, 0, 0, 1)

                def step(h, par, is_first, has_next):
                    base = unit_base(h)
                    slots = step_units(is_first, has_next)
                    if s.wide:
                        own_nth = H // 2 if has_next is None else has_next - par
                        pe.wait_ge(v_in[par], 32 * own_nth)
                    pe.wait_ge(freed, base)
                    for t in range(NT + 1):
                        own = [(score, t, half) for half in range(2)] if t < NT else []
                        own += [(add, t - 1, part) for part in range(2)] if t >= 1 else []
                        units = slots[t] if t < NT else []
                        for k, (what, tile, part) in enumerate(own):
                            what(h, par, tile, part)
                            for u, unit in units[k * len(units) // len(own):(k + 1) * len(units) // len(own)]:
                                if unit[0] == "out":
                                    fill(unit, base, u, 1 - par, h - 1, H // 2 if has_next is None else has_next - 1)
                                else:
                                    fill(unit, base, u, 1 - par, h + 1, has_next)
                    if s.wide:
                        fold(h, base + sum(len(slot) for slot in slots))

                def finish():
                    base = unit_base(H - 1) + first_out
                    for u, unit in enumerate(s.out_units):
                        fill(unit, base, u, 1, H - 1, H // 2)

                run(pe, prepare, step, finish)

            @block.scalar
            def _(act):
                def split_count(h):
                    return s.n_split * h

                def take(unit, base, u, par, h):
                    kind, i, a, n = unit
                    if kind not in "kq":
                        return
                    act.wait_ge(filled, base + u + 1)
                    dst, bias = (k_s, bk_s) if kind == "k" else (q_s, bq_s)
                    again = k2_s if kind == "k" else qm_s
                    nc.scalar.activation(again[par][0:64, a:a + n], work[u % NW][0:64, 0:n], ACT.Identity,
                                         bias=bias[par][0:64, :])
                    nc.scalar.activation(dst[par][:, a:a + n], work[u % NW][:, 0:n], ACT.Identity,
                                         bias=bias[par][:, :]).then_inc(rounded, 1)

                def prepare():
                    for u, unit in enumerate(s.prep_units):
                        take(unit, 0, u, 0, 0)

                def step(h, par, is_first, has_next):
                    base = unit_base(h)
                    slots = step_units(is_first, has_next)
                    for t in range(NT):
                        act.wait_ge(scored, h * NT + t + 1)
                        prev = prev_user(t, s.n_probs)
                        if not (isinstance(h, int) and h == 0 and prev < 0):
                            act.wait_ge(added, h * NT + prev + 1)
                            if s.wide:
                                for half in range(2):
                                    act.wait_ge(summed[half], h * NT + prev + 1)
                        q0 = s.first_query(t)
                        nc.scalar.activation(probs[t % s.n_probs][:, q0:NQ], m.scores[t % 2][:, q0:NQ], ACT.Exp,
                                             bias=mask_bias[:, t:t + 1] if s.masked else 0.0,
                                             scale=s.scale).then_inc(exped, 1)
                        for u, unit in slots[t]:
                            take(unit, base, u, 1 - par, h + 1)
                    act.wait_ge(added, (h + 1) * NT)
                    if not is_first:
                        act.wait_ge(freed, base + first_out)
                    last = nc.scalar.activation(acc_s[:, :], m.sums[0][:, :], ACT.Copy)
                    if s.wide:
                        act.wait_ge(folded, 2 * (h + 1))
                        last = nc.scalar.activation(den_s[:, :], m.sums[1][:, :], ACT.Copy)
                    last.then_inc(acc_taken, 1)

                run(act, prepare, step, lambda: None)

            def sum_probs(engine, namespace, h, t, half):
                engine.wait_ge(exped, h * NT + t + 1)
                if t == 0 and not (isinstance(h, int) and h == 0):
                    engine.wait_ge(folded, 2 * h)
                if t >= 1:
                    engine.wait_ge(summed[half], h * NT + t)
                cols = slice(half * HALF, (half + 1) * HALF)
                p, so_far = probs[t % s.n_probs][:, cols], sum_p[:, cols]
                if t == 0:
                    one = m.ones[:, 0:1].broadcast_to([P, HALF])
                    namespace.tensor_tensor(so_far, p, one, ALU.mult).then_inc(summed[half], 1)
                else:
                    namespace.tensor_tensor(so_far, so_far, p, ALU.add).then_inc(summed[half], 1)

            if s.wide:

                @block.gpsimd
                def _(pool):
                    def step(h, par, is_first, has_next):
                        for t in range(NT):
                            sum_probs(pool, nc.gpsimd, h, t, 0)

                    run(pool, lambda: None, step, lambda: None)

            @block.vector
            def _(dve):
                def take(unit, base, u, par, h):
                    kind, i, a, n = unit
                    bank = work[u % NW]
                    if kind in "kq":
                        dve.wait_ge(rounded, s.n_split * h + i + 1 + (len(s.k_parts) if kind == "q" else 0))
                        bias = bk_s if kind == "k" else bq_s
                        hi = (k_s if kind == "k" else q_s)[par]
                        lo, r = (hi, slice(64, 128)) if kind == "k" else (q2_s[par], slice(0, 64))
                        last = nc.vector.scalar_tensor_tensor(out=lo[r, a:a + n], in0=bank[r, 0:n], scalar=bias[par][r, :],
                                                              in1=hi[r, a:a + n].bitcast(F32), op0=ALU.add,
                                                              op1=ALU.subtract)
                    elif kind == "max":
                        j, c, (a, n) = i, a, n
                        dve.wait_ge(filled, base + u + 1)
                        if not s.wide and j == 0 and c == 0:
                            nc.vector.tensor_copy(v_s[par][:, :, 0:d], v_all[:, :, bass.ds(h * d, d)])
                        last = nc.vector.reduce_max(part_max[:, j, c:c + 1], bank[:, 0:n], AX.X)
                    elif kind == "row":
                        dve.wait_ge(filled, base + u + 1)
                        last = nc.vector.tensor_copy(row_q[par][s.max_at:s.max_at + 1, a:a + n],
                                                     bank[s.max_at:s.max_at + 1, 0:n])
                    else:
                        dve.wait_ge(filled, base + u + 1)
                        g, j0 = len(a), a[0]
                        out = bank[:, 0:g * (D + 1)].rearrange("p (g n) -> p g n", n=D + 1)
                        nc.vector.reciprocal(inv[:, j0:j0 + g], out[:, :, D]).then_inc(inverted, 1)
                        dve.wait_ge(inverted, len(s.out_units) * h + i + 1)
                        for x, j in enumerate(a):
                            last = nc.vector.scalar_tensor_tensor(out=m.x[:, j, :], in0=out[:, x, 0:D],
                                                                  scalar=inv[:, j:j + 1], in1=m.x[:, j, :],
                                                                  op0=ALU.mult, op1=ALU.add)
                    last.then_inc(freed, 1)
                    if kind == "max" and s.last_chunk(j, c):
                        dve.wait_ge(freed, base + u + 1)
                        nc.vector.reduce_max(query_max[:, j:j + 1], part_max[:, j, 0:c + 1], AX.X).then_inc(max_done, 1)

                def prepare():
                    for u, unit in enumerate(s.prep_units):
                        take(unit, 0, u, 0, 0)

                def step(h, par, is_first, has_next):
                    base = unit_base(h)
                    slots = step_units(is_first, has_next)
                    for t in range(NT + 1):
                        if s.wide and t >= 1:
                            sum_probs(dve, nc.vector, h, t - 1, 1)
                        for u, unit in slots[t] if t < NT else []:
                            if unit[0] == "out":
                                take(unit, base, u, 1 - par, h - 1)
                            else:
                                take(unit, base, u, 1 - par, h + 1)

                def finish():
                    base = unit_base(H - 1) + first_out
                    for u, unit in enumerate(s.out_units):
                        take(unit, base, u, 1, H - 1)
                    dve.wait_ge(freed, base + first_out)

                run(dve, prepare, step, finish)


def add_row(m, tag, pieces, plain):
    nc = m.nc
    (spread, s0), (made, m0) = m.shared("row_spread", len(pieces) + 1), m.shared("row_made", 1)
    added, a0 = m.shared("row_added", QT)
    with ExitStack() as ctx:
        cols = m.sb(f"{tag}_cols", [P, max(1, len(pieces)), P], ctx=ctx)
        with nc.Block() as block:

            @block.tensor
            def _(pe):
                pe.wait_ge(spread, s0 + len(pieces) + 1)
                for i, (v, w) in enumerate(pieces):
                    nc.tensor.matmul(m.work[0][:, 0:D], cols[0:v.shape[0], i, :], w, start=(i == 0), stop=False)
                nc.tensor.matmul(m.work[0][:, 0:D], m.ones[0:1, :], plain, start=(not pieces),
                                 stop=True).then_inc(made, 1)

            @block.vector
            def _(dve):
                nc.vector.nop().then_inc(spread, 1)
                for i, (v, w) in enumerate(pieces):
                    nc.vector.tensor_scalar(cols[0:v.shape[0], i, :], m.ones[0:v.shape[0], :], v, None,
                                            ALU.mult).then_inc(spread, 1)
                dve.wait_ge(made, m0 + 1)
                for j in range(QT):
                    nc.vector.tensor_tensor(m.x[:, j, :], m.work[0][:, 0:D], m.x[:, j, :],
                                            ALU.add).then_inc(added, 1)
                dve.wait_ge(added, a0 + QT)


def feed_forward(m, w):
    nc = m.nc
    HID = 4
    with ExitStack() as ctx:
        sb = lambda name, shape, dt=F32: m.sb(name, shape, dt, ctx)
        w1, w2 = sb("f_w1", [D, HID * P]), sb("f_w2", [P, HID, D])
        b1, b2 = sb("f_b1", [P, HID]), sb("f_b2", [P, D])
        hid = sb("f_hid", [P, HID, NQ])
        load_columns(m, "f_in", [(w1[:, :], w["w1"]), (w2[:, :, :], w["w2"].rearrange("(c p) n -> p c n", p=P)),
                                 (b1[:, :], w["b1"].rearrange("(c p) -> p c", p=P)),
                                 (b2[:, :], row(w["b2"]).broadcast_to([P, D]))])
        up, gelu, down, taken = (m.sem(f"f_{s}") for s in ("up", "gelu", "down", "taken"))
        with nc.Block() as block:

            @block.tensor
            def _(pe):
                for c in range(HID):
                    for h in range(2):
                        n = 2 * c + h
                        if n >= 2:
                            pe.wait_ge(gelu, n - 1)
                        nc.tensor.matmul(m.work[n % 2][:, :], w1[:, c * P:(c + 1) * P],
                                         m.x_t[:, h * HALF:(h + 1) * HALF], start=True, stop=True).then_inc(up, 1)
                pe.wait_ge(gelu, 2 * HID)
                for j in range(QT):
                    if j >= 2:
                        pe.wait_ge(taken, 2 * (j - 1))
                    for c in range(HID):
                        last = nc.tensor.matmul(m.sums[j % 2][:, 0:D], hid[:, c, j * P:(j + 1) * P], w2[:, c, :],
                                                start=(c == 0), stop=(c == HID - 1))
                    last.then_inc(down, 1)

            @block.scalar
            def _(act):
                for n in range(2 * HID):
                    c, h = divmod(n, 2)
                    act.wait_ge(up, n + 1)
                    nc.scalar.activation(hid[:, c, h * HALF:(h + 1) * HALF], m.work[n % 2][:, :], ACT.Gelu,
                                         bias=b1[:, c:c + 1]).then_inc(gelu, 1)

            @block.vector
            def _(dve):
                for j in range(QT):
                    dve.wait_ge(down, j + 1)
                    nc.vector.tensor_tensor(m.x[:, j, :], m.sums[j % 2][:, 0:D], m.x[:, j, :],
                                            ALU.add).then_inc(taken, 1)
                    dve.wait_ge(taken, 2 * j + 1)
                    nc.vector.tensor_tensor(m.x[:, j, :], m.x[:, j, :], b2[:, :], ALU.add).then_inc(taken, 1)
                dve.wait_ge(taken, 2 * QT)


def copy_x(m, tag, dst):
    nc = m.nc
    done = m.sem(f"{tag}_done")
    with nc.Block() as block:

        @block.vector
        def _(dve):
            nc.vector.tensor_copy(dst[:, :, :], m.x[:, :, :]).then_inc(done, 1)
            dve.wait_ge(done, 1)


def normalized_queries(m, tag, gain, shift):
    with ExitStack() as ctx:
        rows = m.sb(f"{tag}_rows", [P, QT, D], ctx=ctx)
        cols = m.sb(f"{tag}_gs", [D, 2], ctx=ctx)
        load_columns(m, f"{tag}_gs", [(cols[:, 0:1], column(gain)), (cols[:, 1:2], column(shift))])
        normalize(m, f"{tag}_n", m.x, NQ, rows)
        turn(m, f"{tag}_t", rows, m.x_t, NQ, cols[:, 0:1], cols[:, 1:2])


def scan_layer(m, w, out):
    nc = m.nc
    S = 64
    BLK = 64
    with ExitStack() as ctx:
        sb = lambda name, shape, dt=F32: m.sb(name, shape, dt, ctx)
        w_in, w_in_t, bmat = sb("s_w_in", [D, D]), sb("s_w_in_t", [D, D]), sb("s_bmat", [D, S])
        a_nat, a_t = sb("s_a", [S, S]), sb("s_a_t", [P, S])
        cmat, b_in = sb("s_cmat", [S, D]), sb("s_b_in", [D, 1])
        y_t, u_t = sb("s_y_t", [D, NQ]), sb("s_u_t", [S, NQ])
        h_t = sb("s_h_t", [S, NQ + 1])
        h_blk = sb("s_h_blk", [P, BLK + 1])
        au_t = sb("s_au_t", [S, NQ])
        au_blk = sb("s_au_blk", [S, BLK])
        load_columns(m, "s_in", [(w_in[:, :], w["W_in"]), (bmat[:, :], w["Bmat"]), (a_nat[:, :], w["A"]),
                                 (cmat[:, :], w["Cmat"]), (b_in[:, :], column(w["b_in"]))])
        made, taken = m.sem("s_made"), m.sem("s_taken")
        with nc.Block() as block:

            @block.tensor
            def _(pe):
                nc.tensor.transpose(m.work[0][:, 0:D], w_in[:, :], m.ident[:, :]).then_inc(made, 1)
                nc.tensor.transpose(m.work[1][0:S, 0:S], a_nat[:, :], m.ident[0:S, 0:S]).then_inc(made, 1)
                pe.wait_ge(taken, 4)
                for h in range(2):
                    nc.tensor.matmul(m.work[h][:, :], w_in_t[:, :], m.x_t[:, h * HALF:(h + 1) * HALF], start=True,
                                     stop=True).then_inc(made, 1)
                for h in range(2):
                    pe.wait_ge(taken, 5 + h)
                    nc.tensor.matmul(m.sums[h][0:S, :], bmat[:, :], y_t[:, h * HALF:(h + 1) * HALF], start=True,
                                     stop=True).then_inc(made, 1)
                for h in range(2):
                    pe.wait_ge(taken, 7 + h)
                    nc.tensor.matmul(m.work[h][0:S, :], a_t[0:S, :], u_t[:, h * HALF:(h + 1) * HALF], start=True,
                                     stop=True).then_inc(made, 1)

            @block.vector
            def _(dve):
                nc.vector.memset(a_t[:, :], 0.0).then_inc(taken, 1)
                nc.vector.memset(h_blk[:, :], 0.0).then_inc(taken, 1)
                dve.wait_ge(made, 1)
                nc.vector.tensor_copy(w_in_t[:, :], m.work[0][:, 0:D]).then_inc(taken, 1)
                dve.wait_ge(made, 2)
                dve.wait_ge(taken, 2)
                nc.vector.tensor_copy(a_t[0:S, :], m.work[1][0:S, 0:S]).then_inc(taken, 1)
                for h in range(2):
                    dve.wait_ge(made, 3 + h)
                    nc.vector.tensor_scalar(y_t[:, h * HALF:(h + 1) * HALF], m.work[h][:, :], b_in[:, :], None,
                                            ALU.add).then_inc(taken, 1)
                for h in range(2):
                    dve.wait_ge(made, 5 + h)
                    nc.vector.tensor_copy(u_t[:, h * HALF:(h + 1) * HALF], m.sums[h][0:S, :]).then_inc(taken, 1)
                for h in range(2):
                    dve.wait_ge(made, 7 + h)
                    nc.vector.tensor_copy(au_t[:, h * HALF:(h + 1) * HALF],
                                          m.work[h][0:S, :]).then_inc(taken, 1)
                dve.wait_ge(taken, 10)

        summed, silu_done, u_ready, h_saved = (m.sem(f"s_{n}") for n in ("summed", "silu", "u_ready", "h_saved"))
        with nc.Block() as block:

            @block.tensor
            def _(pe):
                with pe.Fori(0, NQ // BLK) as b:
                    pe.wait_ge(u_ready, b + 1)
                    for i in range(BLK):
                        z = m.work[i % 2][0:S, 0:1]
                        if i >= 1:
                            pe.wait_ge(silu_done, b * BLK + i)
                        nc.tensor.matmul(z, a_t[:, :], h_blk[:, i:i + 1], start=True, stop=True).then_inc(summed, 1)

            @block.scalar
            def _(act):
                with act.Fori(0, NQ // BLK) as b:
                    act.wait_ge(u_ready, b + 1)
                    for i in range(BLK):
                        act.wait_ge(summed, b * BLK + i + 1)
                        nc.scalar.activation(h_blk[0:S, i + 1:i + 2], m.work[i % 2][0:S, 0:1], ACT.Silu,
                                             bias=au_blk[:, i:i + 1]).then_inc(silu_done, 1)

            @block.vector
            def _(dve):
                with dve.Fori(0, NQ // BLK) as b:
                    nc.vector.tensor_copy(au_blk[:, :], au_t[:, bass.ds(b * BLK, BLK)]).then_inc(u_ready, 1)
                    dve.wait_ge(silu_done, (b + 1) * BLK)
                    nc.vector.tensor_copy(h_t[:, bass.ds(b * BLK, BLK + 1)], h_blk[0:S, :]).then_inc(h_saved, 1)
                    dve.wait_ge(h_saved, 2 * b + 1)
                    nc.vector.tensor_copy(h_blk[0:S, 0:1], h_blk[0:S, BLK:BLK + 1]).then_inc(h_saved, 1)
                    dve.wait_ge(h_saved, 2 * b + 2)

        summed_s, put, added, stored = (m.sem(f"s_{n}") for n in ("states", "put", "added", "stored"))
        with nc.Block() as block:

            @block.vector
            def _(dve):
                nc.vector.tensor_tensor(h_t[:, 0:NQ], h_t[:, 0:NQ], u_t[:, :], ALU.add).then_inc(summed_s, 1)
                for j in range(QT):
                    dve.wait_ge(put, j + 1)
                    nc.vector.tensor_tensor(m.x[:, j, :], m.work[j % 2][:, 0:D], m.x[:, j, :],
                                            ALU.add).then_inc(added, 1)

            @block.tensor
            def _(pe):
                pe.wait_ge(summed_s, 1)
                for j in range(QT):
                    if j >= 2:
                        pe.wait_ge(added, j - 1)
                    nc.tensor.matmul(m.work[j % 2][:, 0:D], h_t[:, j * P:(j + 1) * P], cmat[:, :], start=True,
                                     stop=True).then_inc(put, 1)

            @block.sync
            def _(sp):
                sp.wait_ge(added, QT)
                sp.dma_start(out.rearrange("(t p) d -> p t d", p=P), m.x[:, :, :]).then_inc(stored, 16)
                sp.wait_ge(stored, 16)


def program(nc, A, out):
    with ExitStack() as ctx:
        m = Machine(nc, ctx)
        L = [{k[9:]: v for k, v in A.items() if k.startswith(f"L{i}_xattn_")} for i in range(4)]
        x_in = A["x"].rearrange("a s d -> (a s) d")
        ctx_in = A["ctx_1024"].rearrange("a s d -> (a s) d")
        prog_in = A["ctxb_2048x64"].rearrange("a s d -> (a s) d")
        constants(m)
        turn(m, "x_in", m.x, m.x_t, NQ, dram=x_in)
        with ExitStack() as c:
            rows = m.sb("ctx_rows", [P, KT, D], ctx=c)
            turn(m, "ctx_in", rows, m.ctx_t, NK, dram=ctx_in)

        gated_attention(m, dict(L[0], mask=A["mask_BxS_ff1"]), None)

        w1 = L[1]
        with ExitStack() as c:
            masks = {n: m.sb(f"mask_{n}", [P, P], ctx=c) for n in ("later_key", "earlier_query", "all")}
            masked = m.sem("masks_made")
            with nc.Block() as block:

                @block.gpsimd
                def _(pool):
                    for t in masks.values():
                        nc.gpsimd.memset(t[:, :], MASKED).then_inc(masked, 1)
                    pool.wait_ge(masked, 3)
                    nc.gpsimd.affine_select(out=masks["later_key"][:, :], in_=masks["later_key"][:, :],
                                            compare_op=ALU.is_gt, fill=0.0, base=0, pattern=[[1, P]],
                                            channel_multiplier=-1).then_inc(masked, 1)
                    nc.gpsimd.affine_select(out=masks["earlier_query"][:, :], in_=masks["earlier_query"][:, :],
                                            compare_op=ALU.is_gt, fill=0.0, base=0, pattern=[[-1, P]],
                                            channel_multiplier=1).then_inc(masked, 1)
                    pool.wait_ge(masked, 5)

            normalized_queries(m, "ln1", w1["ln1_g"], w1["ln1_b"])
            plain = m.sb("b_self", [1, D], ctx=c)
            load_columns(m, "b_self", [(plain[:, :], row(w1["proj_s_b"]))])
            add_row(m, "add_self", [], plain[:, :])
            head_attention(m, Heads("self", 16, 8, NQ, float(D) ** -0.5, causal=True),
                           dict(Wq=w1["Wq_s"], Wk=w1["Wk_s"], Wv=w1["Wv_s"], Wo=w1["proj_s_w"], bq=None),
                           m.x_t, m.x_t, masks)
        normalized_queries(m, "ln2", w1["ln2_g"], w1["ln2_b"])
        with ExitStack() as c:
            plain = m.sb("b_cross", [1, D], ctx=c)
            load_columns(m, "b_cross", [(plain[:, :], row(w1["proj_c_b"]))])
            add_row(m, "add_cross", [], plain[:, :])
        head_attention(m, Heads("cross", 16, 8, NK, float(D) ** -0.5),
                       dict(Wq=w1["Wq_c"], Wk=w1["Wk_c"], Wv=w1["Wv_c"], Wo=w1["proj_c_w"], bq=None),
                       m.ctx_t, m.x_t)
        normalized_queries(m, "ln3", w1["ln3_g"], w1["ln3_b"])
        feed_forward(m, w1)

        w2 = L[2]
        turn(m, "x2", m.x, m.x_t, NQ)
        with ExitStack() as c:
            wo = m.sb("wo2", [P, 8, D], ctx=c)
            bv = m.sb("bv2", [P, 8], ctx=c)
            bo = m.sb("bo2", [1, D], ctx=c)
            load_columns(m, "wo2", [(wo[:, :, :], w2["Wo"].rearrange("(c p) n -> p c n", p=P)),
                                    (bv[:, :], w2["bv"].rearrange("(c p) -> p c", p=P)), (bo[:, :], row(w2["bo"]))])
            add_row(m, "add2", [(bv[:, i:i + 1], wo[:, i, :]) for i in range(8)], bo[:, :])
        head_attention(m, Heads("wide", 16, 64, NK, 0.125, masked=True), w2, m.ctx_t, m.x_t, A["mask_BxS2_ik0"])
        normalize(m, "post2", m.x, NQ)
        with ExitStack() as c:
            gb = m.sb("gb2", [P, 2, D], ctx=c)
            load_columns(m, "gb2", [(gb[:, 0, :], row(w2["gamma"]).broadcast_to([P, D])),
                                    (gb[:, 1, :], row(w2["beta"]).broadcast_to([P, D]))])
            scaled = m.sem("post2_gained")
            with nc.Block() as block:

                @block.vector
                def _(dve):
                    for j in range(QT):
                        nc.vector.tensor_tensor(m.x[:, j, :], m.x[:, j, :], gb[:, 0, :], ALU.mult).then_inc(scaled, 1)
                    dve.wait_ge(scaled, QT)
                    for j in range(QT):
                        nc.vector.tensor_tensor(m.x[:, j, :], m.x[:, j, :], gb[:, 1, :], ALU.add).then_inc(scaled, 1)
                    dve.wait_ge(scaled, 2 * QT)

        w3 = L[3]
        with ExitStack() as c:
            rows = m.sb("ctx_rows3", [P, KT, D], ctx=c)
            gs = m.sb("gs3", [D, 2], ctx=c)
            loaded = m.sem("ctx3_in")
            with nc.Block() as block:

                @block.sync
                def _(sp):
                    done, count = load_rows(m, "ctx3", ctx_in, rows, NK, sp)
                    sp.dma_start(gs[:, 0:1], column(w3["g1"])).then_inc(loaded, 16)
                    sp.dma_start(gs[:, 1:2], column(w3["beta1"])).then_inc(loaded, 16)
                    sp.wait_ge(done, count)
                    sp.wait_ge(loaded, 32)

            normalize(m, "ctx3n", rows, NK)
            turn(m, "ctx3t", rows, m.ctx_t, NK, gs[:, 0:1], gs[:, 1:2])
        with ExitStack() as c:
            qkv = m.sb("qkv3", [P, 4, D], ctx=c)
            qkv_t = m.sb("qkv3_t", [D, 4 * P], ctx=c)
            load_columns(m, "qkv3", [(qkv[:, 0:3, :], w3["W_qkv"].rearrange("(c p) n -> p c n", p=P)),
                                     (qkv[:, 3, :], w3["W_o"])])
            turn(m, "qkv3t", qkv, qkv_t, 4 * P)
            w_t = nc.dram_tensor("layer3_weights_t", [D, 4 * P], F32, kind="Internal").ap()
            load_columns(m, "qkv3_out", [(w_t, qkv_t[:, :])])
            bv, bo = m.sb("bv3", [P, 1], ctx=c), m.sb("bo3", [1, D], ctx=c)
            load_columns(m, "b3", [(bv[:, :], column(w3["b_qkv"][2 * D:3 * D])), (bo[:, :], row(w3["b_o"]))])
            normalized_queries(m, "ln4", w3["g1"], w3["beta1"])
            add_row(m, "add3", [(bv[:, :], qkv_t[:, 3 * D:4 * D])], bo[:, :])
        head_attention(m, Heads("last", 8, 16, NK, 0.25),
                       dict(Wq=w_t[:, 0:D], Wk=w_t[:, D:2 * D], Wv=w_t[:, 2 * D:3 * D], Wo=w_t[:, 3 * D:4 * D],
                            bq=w3["b_qkv"][0:D], bk=w3["b_qkv"][D:2 * D]), m.ctx_t, m.x_t)
        normalized_queries(m, "ln5", w3["g2"], w3["beta2"])
        with ExitStack() as c:
            prog = m.sb("prog", [P, KT, 64], ctx=c)
            w_prog, w_prog_t = m.sb("w_prog", [P, 64], ctx=c), m.sb("w_prog_t", [64, D], ctx=c)
            mean, b_prog = m.sb("prog_mean", [64, 1], ctx=c), m.sb("b_prog", [1, D], ctx=c)
            load_columns(m, "prog", [(prog[:, 0:FULL, :], prog_in[0:FULL * P, :].rearrange("(t p) d -> p t d", p=P)),
                                     (prog[0:TAIL, FULL, :], prog_in[FULL * P:NK, :]),
                                     (w_prog[:, :], w3["W_prog"]), (b_prog[:, :], row(w3["b_prog"]))])
            made, copied = m.sem("prog_made"), m.sem("prog_copied")
            with nc.Block() as block:

                @block.tensor
                def _(pe):
                    for t in range(KT):
                        r = P if t < FULL else TAIL
                        last = nc.tensor.matmul(m.work[0][0:64, 0:1], prog[0:r, t, :], m.ones[0:r, 0:1],
                                                start=(t == 0), stop=(t == KT - 1))
                    last.then_inc(made, 1)
                    nc.tensor.transpose(m.work[1][0:64, 0:D], w_prog[:, :], m.ident[:, :]).then_inc(made, 1)

                @block.vector
                def _(dve):
                    dve.wait_ge(made, 2)
                    nc.vector.tensor_scalar(mean[:, :], m.work[0][0:64, 0:1], 1.0 / NK, None, ALU.mult).then_inc(copied, 1)
                    nc.vector.tensor_copy(w_prog_t[:, :], m.work[1][0:64, 0:D]).then_inc(copied, 1)
                    dve.wait_ge(copied, 2)

            add_row(m, "add_prog", [(mean[:, :], w_prog_t[:, :])], b_prog[:, :])
        scan_layer(m, w3, out.rearrange("a s d -> (a s) d"))


_UNUSED = ("itok_BxS2_4_31999",)


def kernel(**inputs):
    import numpy as _np
    import concourse.bacc as _bacc
    from concourse import mybir as _mybir
    from concourse.bass_utils import run_bass_kernel_spmd as _run

    nc = _bacc.Bacc("TRN2", target_bir_lowering=False, num_devices=1)
    arrays, args = {}, {}
    for name, value in inputs.items():
        if name in _UNUSED:
            continue
        a = _np.ascontiguousarray(value)
        arrays[f"in_{name}"] = a
        args[name] = nc.dram_tensor(f"in_{name}", a.shape, _mybir.dt.from_np(a.dtype), kind="ExternalInput").ap()
    out = nc.dram_tensor("out", (1, NQ, D), F32, kind="ExternalOutput").ap()
    program(nc, args, out)
    r = _run(nc, [arrays], core_ids=[0])
    return r.results[0]["out"]
```
